# Optimizing a Trainium2 kernel written in Bass

```python
import numpy as np
import jax
import jax.numpy as jnp

def _softmax(x, axis=-1):
    return jax.nn.softmax(x, axis=axis)

def _gelu(x):
    return jax.nn.gelu(x, approximate=True)

def _silu(x):
    return jax.nn.silu(x)

def _sigmoid(x):
    return jax.nn.sigmoid(x)

def _layernorm(x, axis=-1, eps=1e-05):
    m = jnp.mean(x, axis=axis, keepdims=True)
    v = jnp.var(x, axis=axis, keepdims=True)
    return (x - m) / jnp.sqrt(v + eps)

def _scatter_add(tgt, idx, src, axis=0):
    return tgt.at[idx].add(src)

def _segment_sum(src, seg, n):
    return jax.ops.segment_sum(src, seg, n)
kernel_name = 'mk_gps_d1_gnn_r16_e0ccb0'

def setup_inputs(seed: int=0):
    np.random.seed(seed)
    _w = jnp.asarray

    def _rec_inputs():
        import jax
        import jax.numpy as jnp
        _gk = jax.random.key(seed)
        x = -0.0001394 + 0.9999 * jax.random.normal(jax.random.fold_in(_gk, 1), (3125, 768), jnp.float32)
        src = jax.random.randint(jax.random.fold_in(_gk, 2), (50000,), 0, 3125, jnp.int32)
        dst = jax.random.randint(jax.random.fold_in(_gk, 3), (50000,), 0, 3125, jnp.int32)
        _o = jnp.argsort(dst, stable=True)
        src = src[_o]
        dst = dst[_o]
        return (x, src, dst)
    x, src, dst = _rec_inputs()

    def _L0_gnn_setup():
        import jax, jax.numpy as jnp
        import numpy as np
        N_NODES = 3125

        def gcn_conv(x, edge_index, W, b, n_nodes):
            src = edge_index[0]
            dst = edge_index[1]
            loop = jnp.arange(n_nodes, dtype=src.dtype)
            src = jnp.concatenate([src, loop])
            dst = jnp.concatenate([dst, loop])
            deg = jax.ops.segment_sum(jnp.ones(src.shape, x.dtype), dst, num_segments=n_nodes)
            dinv = jnp.where(deg > 0, jax.lax.rsqrt(deg), jnp.zeros_like(deg))
            norm = dinv[src] * dinv[dst]
            h = x @ W.T
            msg = h[src] * norm[:, None]
            out = jax.ops.segment_sum(msg, dst, num_segments=n_nodes)
            return out + b
        key = jax.random.key(seed)
        k1, k2, k3, k4 = jax.random.split(key, 4)
        d = 768
        n_edges = 12500
        s = 1.0 / np.sqrt(d)
        return {'x': jax.random.normal(k1, (N_NODES, d), dtype=jnp.float32), 'edge_index': jax.random.randint(k2, (2, n_edges), 0, N_NODES, dtype=jnp.int64), 'W1': jax.random.normal(k3, (d, d), dtype=jnp.float32) * s, 'b1': jnp.zeros((d,), jnp.float32), 'W2': jax.random.normal(k4, (d, d), dtype=jnp.float32) * s, 'b2': jnp.zeros((d,), jnp.float32)}
    _L0_gnn_all = _L0_gnn_setup()
    _L0_gnn_in = {k: v for k, v in _L0_gnn_all.items() if k in ('W1', 'b1', 'W2', 'b2')}
    del _L0_gnn_all

    def _L0_mix_setup():
        import jax, jax.numpy as jnp
        import numpy as np
        import math
        B, N, C = (8, 256, 768)
        H = 12
        DH = C // H
        M = 256
        LN_EPS = 1e-05

        def _phi(t, random_features):
            norm_sq = 0.5 * jnp.sum(t * t, axis=-1, keepdims=True)
            proj = jnp.einsum('bhnd,md->bhnm', t, random_features)
            return jnp.exp(proj - norm_sq) * (1.0 / math.sqrt(M))
        key = jax.random.key(seed)
        ks = jax.random.split(key, 7)
        x = jax.random.normal(ks[0], (B, N, C), dtype=jnp.float32)
        W_qkv = jax.random.normal(ks[1], (C, 3 * C), dtype=jnp.float32) * (1.0 / math.sqrt(C))
        W_proj = jax.random.normal(ks[2], (C, C), dtype=jnp.float32) * (1.0 / math.sqrt(C))
        b_proj = jnp.zeros((C,), dtype=jnp.float32)
        gamma = jnp.ones((C,), dtype=jnp.float32)
        beta = jnp.zeros((C,), dtype=jnp.float32)
        random_features = jax.random.normal(ks[3], (M, DH), dtype=jnp.float32) / math.sqrt(DH)
        return {'x': x, 'W_qkv': W_qkv, 'W_proj': W_proj, 'b_proj': b_proj, 'gamma': gamma, 'beta': beta, 'random_features': random_features}
    _L0_mix_all = _L0_mix_setup()
    _L0_mix_in = {k: v for k, v in _L0_mix_all.items() if k in ('W_qkv', 'W_proj', 'b_proj', 'gamma', 'beta', 'random_features')}
    del _L0_mix_all

    def _L0_ffn_setup():
        import jax, jax.numpy as jnp
        import numpy as np
        from jax import lax
        H = 768
        I = 128
        E = 8
        K = 2
        key = jax.random.key(seed)
        k1, k2, k3, k4 = jax.random.split(key, 4)
        x = jax.random.normal(k1, (1, 1024, H), dtype=jnp.float32)
        router_w = jax.random.normal(k2, (E, H), dtype=jnp.float32) * (1.0 / np.sqrt(H))
        w1 = jax.random.normal(k3, (E, H, I), dtype=jnp.float32) * (1.0 / np.sqrt(H))
        w2 = jax.random.normal(k4, (E, I, H), dtype=jnp.float32) * (1.0 / np.sqrt(I))
        return {'x': x, 'router_w': router_w, 'w1': w1, 'w2': w2}
    _L0_ffn_all = _L0_ffn_setup()
    _L0_ffn_in = {k: v for k, v in _L0_ffn_all.items() if k in ('router_w', 'w1', 'w2')}
    del _L0_ffn_all
    return {'x': x, 'src': src, 'dst': dst, 'L0_gnn_W1': _L0_gnn_in['W1'], 'L0_gnn_b1': _L0_gnn_in['b1'], 'L0_gnn_W2': _L0_gnn_in['W2'], 'L0_gnn_b2': _L0_gnn_in['b2'], 'L0_mix_W_qkv': _L0_mix_in['W_qkv'], 'L0_mix_W_proj': _L0_mix_in['W_proj'], 'L0_mix_b_proj': _L0_mix_in['b_proj'], 'L0_mix_gamma': _L0_mix_in['gamma'], 'L0_mix_beta': _L0_mix_in['beta'], 'L0_mix_random_features': _L0_mix_in['random_features'], 'L0_ffn_router_w': _L0_ffn_in['router_w'], 'L0_ffn_w1': _L0_ffn_in['w1'], 'L0_ffn_w2': _L0_ffn_in['w2']}

def reference(x, src, dst, L0_gnn_W1, L0_gnn_b1, L0_gnn_W2, L0_gnn_b2, L0_mix_W_qkv, L0_mix_W_proj, L0_mix_b_proj, L0_mix_gamma, L0_mix_beta, L0_mix_random_features, L0_ffn_router_w, L0_ffn_w1, L0_ffn_w2):
    import jax
    import jax.numpy as jnp

    def _L0_gnn_ref(x, edge_index, W1, b1, W2, b2):
        import jax, jax.numpy as jnp
        import numpy as np
        N_NODES = 3125

        def gcn_conv(x, edge_index, W, b, n_nodes):
            src = edge_index[0]
            dst = edge_index[1]
            loop = jnp.arange(n_nodes, dtype=src.dtype)
            src = jnp.concatenate([src, loop])
            dst = jnp.concatenate([dst, loop])
            deg = jax.ops.segment_sum(jnp.ones(src.shape, x.dtype), dst, num_segments=n_nodes)
            dinv = jnp.where(deg > 0, jax.lax.rsqrt(deg), jnp.zeros_like(deg))
            norm = dinv[src] * dinv[dst]
            h = x @ W.T
            msg = h[src] * norm[:, None]
            out = jax.ops.segment_sum(msg, dst, num_segments=n_nodes)
            return out + b
        h = gcn_conv(x, edge_index, W1, b1, N_NODES)
        h = jax.nn.relu(h)
        out = gcn_conv(h, edge_index, W2, b2, N_NODES)
        return out

    def _L0_mix_ref(x, W_qkv, W_proj, b_proj, gamma, beta, random_features):
        import jax, jax.numpy as jnp
        import numpy as np
        import math
        B, N, C = (8, 256, 768)
        H = 12
        DH = C // H
        M = 256
        LN_EPS = 1e-05

        def _phi(t, random_features):
            norm_sq = 0.5 * jnp.sum(t * t, axis=-1, keepdims=True)
            proj = jnp.einsum('bhnd,md->bhnm', t, random_features)
            return jnp.exp(proj - norm_sq) * (1.0 / math.sqrt(M))
        b, n, c = x.shape
        qkv = (x @ W_qkv).reshape(b, n, 3, H, DH)
        qkv = jnp.transpose(qkv, (2, 0, 3, 1, 4))
        q, k, v = (qkv[0], qkv[1], qkv[2])
        q_p = _phi(q, random_features)
        k_p = _phi(k, random_features)
        kv = jnp.einsum('bhnm,bhnd->bhmd', k_p, v)
        out = jnp.einsum('bhnm,bhmd->bhnd', q_p, kv)
        k_sum = jnp.sum(k_p, axis=2)
        normalizer = jnp.einsum('bhnm,bhm->bhn', q_p, k_sum)[..., None]
        out = out / (normalizer + 1e-06)
        x_attn = jnp.transpose(out, (0, 2, 1, 3)).reshape(b, n, c)
        x_attn = x_attn @ W_proj + b_proj
        y = x + x_attn
        mu = jnp.mean(y, axis=-1, keepdims=True)
        var = jnp.mean(jnp.square(y - mu), axis=-1, keepdims=True)
        return (y - mu) * jax.lax.rsqrt(var + LN_EPS) * gamma + beta

    def _L0_ffn_ref(x, router_w, w1, w2):
        import jax, jax.numpy as jnp
        import numpy as np
        from jax import lax
        H = 768
        I = 128
        E = 8
        K = 2
        B, S, _ = x.shape
        xt = x.reshape(-1, H)
        logits = xt @ router_w.T
        probs = jax.nn.softmax(logits, axis=-1)
        top_w, top_i = lax.top_k(probs, K)
        top_w = top_w / jnp.sum(top_w, axis=-1, keepdims=True)
        e_sel = jnp.max(top_i, axis=-1)

        def step(out, inp):
            idx, W1e, W2e = inp
            y = jax.nn.silu(xt @ W1e) @ W2e
            mask = (e_sel == idx)[:, None]
            return (jnp.where(mask, y, out), None)
        out0 = jnp.zeros_like(xt)
        out, _ = lax.scan(step, out0, (jnp.arange(E), w1, w2))
        return out.reshape(B, S, H)
    edge_index = jnp.stack([src, dst])
    xn = _layernorm(x, axis=-1)
    x = x + _L0_gnn_ref(xn, edge_index, L0_gnn_W1, L0_gnn_b1, L0_gnn_W2, L0_gnn_b2) + _L0_mix_ref(xn[None], L0_mix_W_qkv, L0_mix_W_proj, L0_mix_b_proj, L0_mix_gamma, L0_mix_beta, L0_mix_random_features)[0]
    x = x + _L0_ffn_ref(_layernorm(x, axis=-1)[None], L0_ffn_router_w, L0_ffn_w1, L0_ffn_w2)[0]
    return x

_drawn_inputs = setup_inputs


def setup_inputs(seed=0):
    import zlib

    import numpy as np

    out = dict(_drawn_inputs(seed))
    spreads = {'L0_gnn_b1': (0.0, 0.1),
     'L0_gnn_b2': (0.0, 0.1),
     'L0_mix_b_proj': (0.0, 0.1),
     'L0_mix_gamma': (1.0, 0.2),
     'L0_mix_beta': (0.0, 0.1)}
    factors = {'L0_mix_W_qkv': 8.0, 'L0_mix_W_proj': 8.0, 'L0_mix_random_features': 8.0}
    for name, (base, spread) in spreads.items():
        noise = np.random.default_rng([zlib.crc32(name.encode()), seed]).standard_normal(out[name].shape)
        drawn = base * np.exp(spread * noise) if base else spread * noise
        out[name] = jnp.asarray(drawn.astype(out[name].dtype))
    for name, factor in factors.items():
        out[name] = (out[name] * factor).astype(out[name].dtype)
    return out
```

```python
from contextlib import ExitStack

import numpy as np

import concourse.bass as bass
from concourse import mybir

F32 = mybir.dt.float32
F16 = mybir.dt.float16
I32 = mybir.dt.int32
ALU = mybir.AluOpType
ACT = mybir.ActivationFunctionType
AXX = mybir.AxisListType.X

P = 128
N = 3125
D = 768
T = -(-N // P)
NP = T * P
K = D // P
HD = D // 2
H, DH, M = 12, 64, 256
PAIRS = H // 2
TC = 5
C = T // TC
CW = TC * P
HW = CW // 2
VW = DH + 2
UNITS = C * PAIRS
E = 50000
EPU = 14
ET = UNITS * EPU
G = 2
EARLIER = 1024.0
NX, NI = 8, 128
HB = NX * NI
CELLS = NP * NP
FAR = float(1 << 24)
LN_EPS = 1e-5
COUNT_EXACT = 2048.0


def over_tiles(eng, body, last=T):
    body(0, 0, 0)
    body(1, 1, 0)
    body(2, 0, 1)
    with eng.Fori(0, (last - 3) // 2) as i:
        body(2 * i + 3, 1, i + 1)
        body(2 * i + 4, 0, i + 2)


def reused(i):
    return not isinstance(i, int) or i > 0


class Chain:

    def __init__(self, eng, sem, base=0):
        self.eng, self.sem, self.n, self.base = eng, sem, 0, base

    def link(self, ins):
        self.n += 1
        ins.then_inc(self.sem, 1)
        self.eng.wait_ge(self.sem, self.base + self.n)


def build(nc, x, src_row, dst_row, src_col, dst_col, w_qkv, w_proj, b_proj, gamma, beta, rf_t,
          g1_t, b1, g2_t, b2, ffn_in, ffn_out, out):
    ctx = ExitStack()
    with ctx:
        sem = lambda name: ctx.enter_context(nc.semaphore(name))
        dram = lambda name, shape, dt=F32: nc.dram_tensor(name, shape, dt, kind="Internal").ap()

        cells = dram("cells", [CELLS, 1])
        cells_t = cells.rearrange("(t p f) o -> t p (f o)", t=T, p=P)
        key_dram = dram("key_dram", [UNITS, EPU * P])
        xn_dram = dram("xn_dram", [NP, D])
        y_dram = dram("y_dram", [NP, D])
        x2_dram = dram("x2_dram", [NP, D])
        hhi_dram = dram("hhi_dram", [NP, D], F16)
        hlo_dram = dram("hlo_dram", [NP, D], F16)

        arena = ctx.enter_context(nc.sbuf_tensor("arena", [P, 53000], F32))

        def at(off, *shape, dt=F32):
            n = int(np.prod(shape))
            if dt == F16:
                ap = arena[:, off:off + (n + 1) // 2].bitcast(F16)[:, 0:n]
            else:
                ap = arena[:, off:off + n]
                if dt != F32:
                    ap = ap.bitcast(dt)
            if len(shape) == 2:
                ap = ap.rearrange("p (a b) -> p a b", a=shape[0])
            if len(shape) == 3:
                ap = ap.rearrange("p (a b c) -> p a b c", a=shape[0], b=shape[1])
            return ap

        RX, RT, RW, WST, RS = 0, 19200, 38400, 47616, 50688
        s_at = [RS]

        def small(*shape, dt=F32):
            n = int(np.prod(shape))
            n = (n + 1) // 2 if dt == F16 else n
            off = s_at[0]
            s_at[0] += n
            assert s_at[0] <= 53000
            return at(off, *shape, dt=dt)

        rfa, rfb = small(M), small(M)
        ident = small(P, dt=F16)
        iota = small(P, dt=F16)
        earlier = small(G, G * P)
        dst_lo16, dst_hi16 = small(ET, dt=F16), small(ET, dt=F16)
        valid = small(T)
        ones60 = small(TC * H)
        iota8 = small(NX)
        deg = small(26)
        dinv = small(T)
        epsb = small(2)
        mvy = small(T, 2)
        ry = small(T)
        mv2 = small(T, 2)
        r2 = small(T)
        t25 = small(4, T)
        sums = small(EPU)
        skip = small(EPU)
        bst = small(2, 12)
        mvt = small(TC, 2)
        bits = small(2, 16)
        flag_f, flag_i = small(2), small(2, dt=I32)
        stage = [at(WST + 1536 * u, 1536) for u in range(2)]

        kcol, idx_all, val_all = at(RX, ET), at(RX + 420, ET, dt=I32), at(RX + 840, ET)
        idx_b, val_b = at(RX + 1260, EPU, dt=I32), at(RX + 1274, EPU)
        eint = [at(RX + 1300 + ET * i, ET, dt=I32) for i in range(8)]
        krow = at(RX + 4660, ET)
        ktmp = at(RX + 5080, ET)
        zeros = at(RX + 5500, NP)
        x_in = [at(RX + 8700 + D * u, D) for u in range(2)]
        xn = [at(RX + 10236 + D * u, D) for u in range(2)]
        xhi = [at(RX + 11772 + HD * u, D, dt=F16) for u in range(2)]
        xlo = [at(RX + 12540 + HD * u, D, dt=F16) for u in range(2)]
        xT = [at(RT + 9600 * part, K, NP, dt=F16) for part in range(2)]
        kk = [at(RX + 1300 + 2 * CW * u, 2, CW) for u in range(2)]
        kp_sb = [at(RX + 3860 + 512 * u, 512) for u in range(2)]
        junk = [at(RX + 4900 + G * P * u, G * P) for u in range(2)]
        kb = [at(RX + 8700 + EPU * P * u, EPU * P) for u in range(2)]
        oh_lo = at(RX + 12284, EPU, P, dt=F16)
        oh_hi = at(RX + 13180, EPU, 26, dt=F16)
        vals = at(RX + 13400, TC, H, VW)
        kv = at(RX + 17430, PAIRS, 4, VW)
        qp_sb = [at(RX + 3860 + 4 * CW * u, 4, CW) for u in range(2)]
        attn = at(RX + 8980, TC, D)
        ahi = [at(RX + 12820 + HD * u, D, dt=F16) for u in range(2)]
        alo = [at(RX + 13588 + HD * u, D, dt=F16) for u in range(2)]
        aT = [[at(RX + 14356 + HD * (2 * part + u), D, dt=F16) for u in range(2)] for part in range(2)]
        xl3 = [at(RX + 15892 + D * u, D) for u in range(2)]
        y_sb = [at(WST + D * u, D) for u in range(2)]
        brow3 = at(WST + 1536, D)
        rden = at(WST + 2304, TC, 2)
        X = [at(RX + 9600 * part, T, D, dt=F16) for part in range(2)]
        a_in = [at(RT + NP * u, NP) for u in range(2)]
        a_hi = [at(RT + 6400 + 1600 * u, T, P, dt=F16) for u in range(2)]
        a_lo = [at(RT + 9600 + 1600 * u, T, P, dt=F16) for u in range(2)]
        ghi = [at(RT + 12800 + HD * u, D, dt=F16) for u in range(2)]
        glo = [at(RT + 13568 + HD * u, D, dt=F16) for u in range(2)]
        gT = [[at(RT + 14336 + HD * (2 * part + u), D, dt=F16) for u in range(2)] for part in range(2)]
        zt = [at(RT + 15872 + D * u, D) for u in range(2)]
        zr = [at(RT + 17408 + D * u, D) for u in range(2)]
        gnn_w = lambda k, part: at(RW + 768 * k + HD * part, D, dt=F16)
        zhi = [at(RW + 4608 + HD * u, D, dt=F16) for u in range(2)]
        zlo = [at(RW + 5376 + HD * u, D, dt=F16) for u in range(2)]
        xl = [at(RW + 6144 + D * u, D) for u in range(2)]
        yl = [at(RW + 7680 + D * u, D) for u in range(2)]
        row_a, row_g = at(WST, D), at(WST + D, D)
        row_t = at(WST + 2 * D, D)
        w_in = lambda k, part: at(RT + 1032 * k + 516 * part, HB + NX, dt=F16)
        w_out = lambda e, part: at(RT + 6192 + 768 * e + HD * part, D, dt=F16)
        fx = [at(RX + D * u, D) for u in range(2)]
        fr = [at(RX + D * (2 + u), D) for u in range(2)]
        fn = [at(RX + 3072 + D * u, D) for u in range(2)]
        fhi = [at(RX + 4608 + HD * u, D, dt=F16) for u in range(2)]
        flo = [at(RX + 5376 + HD * u, D, dt=F16) for u in range(2)]
        fT = [[at(RX + 6144 + HD * (2 * part + u), D, dt=F16) for u in range(2)] for part in range(2)]
        hsel_all = at(RX + 7680, NX, NI)
        hsel, hact = at(RX + 8704, NI), at(RX + 8832, NI)
        act_hi, act_lo = at(RX + 8960, NI, dt=F16), at(RX + 9024, NI, dt=F16)
        m_hi, m_lo = at(RX + 9088, NX, NI, dt=F16), at(RX + 9600, NX, NI, dt=F16)
        mT = [[at(RX + 10112 + 512 * (2 * part + u), HB, dt=F16) for u in range(2)] for part in range(2)]
        fo = [at(RX + 12160 + D * u, D) for u in range(2)]
        lg, top, mask = at(RX + 13700, NX), at(RX + 13708, NX), at(RX + 13716, NX)
        topi = at(RX + 13724, NX, dt=mybir.dt.uint32)
        topf, esel, mask16 = at(RX + 13732, NX), at(RX + 13740, 2), at(RX + 13744, NX, dt=F16)
        nmax = at(RX + 13750, 2)

        pair = [ctx.enter_context(nc.psum_tensor(f"pair{i}", [P, 2, 512], F32)) for i in range(4)]
        bank = lambda b: pair[b // 2][:, b % 2, :]
        bank16 = lambda b: pair[b // 2][:, b % 2, :].bitcast(F16)
        wide = lambda i: pair[i][:, :, 0:HD]
        halves = lambda ap: ap.rearrange("p (a b) -> p a b", a=2)

        KV_W, QP_W, G1_W, G2_W, FIN_W, FOUT_W = range(6)
        items = []
        for k in range(K):
            off = RW + 1536 * k
            items.append((KV_W, w_qkv[k * P:(k + 1) * P, D:3 * D], 2 * D,
                          at(off, 2 * D, dt=F16), at(off + D, 2 * D, dt=F16)))
        for j, w in enumerate((w_qkv[:, 0:D], w_proj)):
            for k in range(K):
                off = RW + 4608 * j + 768 * k
                items.append((QP_W, w[k * P:(k + 1) * P, :], D, at(off, D, dt=F16), at(off + HD, D, dt=F16)))
        for seg, w in ((G1_W, g1_t), (G2_W, g2_t)):
            for k in range(K):
                items.append((seg, w[k * P:(k + 1) * P, :], D, gnn_w(k, 0), gnn_w(k, 1)))
        for k in range(K):
            items.append((FIN_W, ffn_in[k * P:(k + 1) * P, :], HB + NX, w_in(k, 0), w_in(k, 1)))
        for e in range(NX):
            items.append((FOUT_W, ffn_out[e * P:(e + 1) * P, :], D, w_out(e, 0), w_out(e, 1)))
        kv_w = lambda k, part: items[k][3 + part]
        q_w = lambda k, part: items[K + k][3 + part]
        p_w = lambda k, part: items[2 * K + k][3 + part]

        w_in_sem = [sem("w_in0"), sem("w_in1")]
        w_hi_done, w_lo_done = sem("w_hi_done"), sem("w_lo_done")

        def load_weights(sp, *segs):
            for m, (seg, src, n, _, _) in enumerate(items):
                if seg in segs:
                    if m >= 2:
                        sp.wait_ge(w_lo_done, m - 1)
                    sp.dma_start(stage[m % 2][:, 0:n], src).then_inc(w_in_sem[m % 2], 16)

        def split_hi(act, *segs):
            for m, (seg, _, n, hi, _) in enumerate(items):
                if seg in segs:
                    act.wait_ge(w_in_sem[m % 2], 16 * (m // 2 + 1))
                    nc.scalar.copy(hi, stage[m % 2][:, 0:n]).then_inc(w_hi_done, 1)

        def split_lo(dve, *segs):
            for m, (seg, _, n, hi, lo) in enumerate(items):
                if seg in segs:
                    dve.wait_ge(w_hi_done, m + 1)
                    nc.vector.tensor_tensor(lo, stage[m % 2][:, 0:n], hi, ALU.subtract).then_inc(w_lo_done, 1)

        def weights_ready(eng, seg):
            eng.wait_ge(w_lo_done, 1 + max(m for m, it in enumerate(items) if it[0] == seg))

        phase_done = sem("phase_done")
        consts, consts_in, zeros_ready = sem("consts"), sem("consts_in"), sem("zeros_ready")
        edges_in, key_made, key_stored = sem("edges_in"), sem("key_made"), sem("key_stored")
        cleared, scattered = sem("cleared"), sem("scattered")
        x_ld = [sem("x_ld0"), sem("x_ld1")]
        xn_st = [sem("xn_st0"), sem("xn_st1")]
        var_ready, sd_ready, xn_ready = sem("var_ready"), sem("sd_ready"), sem("xn_ready")
        hi_ready, lo_ready, tr_done = sem("hi_ready"), sem("lo_ready"), sem("tr_done")
        ev_hi, ev_lo = sem("ev_hi"), sem("ev_lo")
        dve_done, mvy_done = sem("dve_done"), sem("mvy_done")
        dve_links = [0]

        def links(each, times=1):
            dve_links[0] += each * times
            return dve_links[0] - each * times

        slot_full = [sem("slot_full0"), sem("slot_full1")]
        slot_free = [sem("slot_free0"), sem("slot_free1")]
        v_ready, vone_ready, kk_sq, kk_cp = sem("v_ready"), sem("vone_ready"), sem("kk_sq"), sem("kk_cp")
        kp_full, kp_exp, kv_full, kv_free = sem("kp_full"), sem("kp_exp"), sem("kv_full"), sem("kv_free")
        kb_in, scan_done = [sem("kb_in0"), sem("kb_in1")], sem("scan_done")
        unit_scanned, pool_copied, idx_ready = sem("unit_scanned"), sem("pool_copied"), sem("idx_ready")
        oh_ready, deg_full, deg_free = sem("oh_ready"), sem("deg_full"), sem("deg_free")

        spacer = {}

        def finish_phase(eng, k):
            eng.drain().then_inc(phase_done, 1)
            eng.wait_ge(phase_done, 4 * (k + 1))

        def apart(eng):
            eng.sem_inc(spacer[eng], 1)

        def mm_split(dst, left, right, k, start, stop):
            for n, (a, b) in enumerate(((0, 0), (0, 1), (1, 0))):
                for half in range(2):
                    ins = nc.tensor.matmul(dst[half], left(k, a), right(k, b, half),
                                           start=start and n == 0, stop=stop and n == 2)
            return ins

        def bank_halves(i, width):
            return [pair[i][:, h, 0:width] for h in range(2)]

        slot_use, uses = {}, [0, 0]
        for n, key in enumerate([("v", t) for t in range(TC)] + [("k", p) for p in range(PAIRS)]):
            slot_use[key] = (n % 2, uses[n % 2])
            uses[n % 2] += 1

        q_use, q_uses = {}, [0, 0]
        for n, key in enumerate([("q", p, g) for p in range(PAIRS) for g in range(4)] + [("y", t) for t in range(TC)]):
            q_use[key] = (n % 2, q_uses[n % 2])
            q_uses[n % 2] += 1
        y_use, y_uses = {}, [0, 0]
        for t in range(TC):
            y_use[t] = (t % 2, y_uses[t % 2])
            y_uses[t % 2] += 1
        qt_full, qt_free, qq_sq, qq_cp = sem("qt_full"), sem("qt_free"), sem("qq_sq"), sem("qq_cp")
        qp_full, qp_free = [sem("qp_full0"), sem("qp_full1")], [sem("qp_free0"), sem("qp_free1")]
        qp_exp, o_full, attn_done = sem("qp_exp"), sem("o_full"), sem("attn_done")
        kv_scaled, vals_clear = sem("kv_scaled"), sem("vals_clear")
        ahi_ready, alo_ready, atr_full = sem("ahi_ready"), sem("alo_ready"), sem("atr_full")
        aT_hi, aT_lo = sem("aT_hi"), sem("aT_lo")
        xl_in, xl_used = [sem("xl_in0"), sem("xl_in1")], [sem("xl_used0"), sem("xl_used1")]
        y_ready, y_st = sem("y_ready"), [sem("y_st0"), sem("y_st1")]
        rows_in = sem("rows_in")
        pre_ld = [sem("pre_ld0"), sem("pre_ld1")]
        pre_hi, pre_lo, pre_sc = sem("pre_hi"), sem("pre_lo"), sem("pre_sc")
        sq_asked, sq_done, flag_max, flag_ready = sem("sq_asked"), sem("sq_done"), sem("flag_max"), sem("flag_ready")
        X_in = [sem(f"X_in{c}") for c in range(C)]

        class Layer:
            def __init__(self, name):
                s = lambda what: sem(f"{name}_{what}")
                self.a_ld = [s("a_ld0"), s("a_ld1")]
                self.ahi, self.alo, self.g_full = s("ahi"), s("alo"), s("g_full")
                self.ghi, self.glo, self.tr = s("ghi"), s("glo"), s("tr")
                self.gT_hi, self.gT_lo, self.z_full, self.z_ev = s("gT_hi"), s("gT_lo"), s("z_full"), s("z_ev")
                self.relu, self.zhi, self.zlo = s("relu"), s("zhi"), s("zlo")
                self.st = [s("st0"), s("st1")]
                self.x_ld = [s("x_ld0"), s("x_ld1")]
                self.done = s("done")

        L1, L2 = Layer("l1"), Layer("l2")
        f_ld, fr_ld = [sem("f_ld0"), sem("f_ld1")], [sem("fr_ld0"), sem("fr_ld1")]
        f_norm, f_hi, f_lo, f_tr, fT_hi, fT_lo = [sem(f"f_{n}") for n in ("norm", "hi", "lo", "tr", "T_hi", "T_lo")]
        f_h, f_hsel, f_act, f_ahi, f_mask, f_mtr = [sem(f"f_{n}") for n in ("h", "hsel", "act", "ahi", "mask", "mtr")]
        mT_hi, mT_lo, f_y, f_out = sem("mT_hi"), sem("mT_lo"), sem("f_y"), sem("f_out")
        f_st = [sem("f_st0"), sem("f_st1")]

        block = ctx.enter_context(nc.Block())

        @block.sync
        def _(sp):
            spacer[sp] = sem("sp_spacer")
            for i, a in enumerate((src_row, dst_row, src_col, dst_col)):
                sp.dma_start(eint[2 * i], a).then_inc(edges_in, 16)
            sp.dma_start(rfa[0:DH, :], rf_t).then_inc(consts_in, 16)
            sp.dma_start(rfb[DH:P, :], rf_t).then_inc(consts_in, 16)
            for u in range(2):
                sp.dma_start(x_in[u], x[u * P:(u + 1) * P, :]).then_inc(x_ld[u], 16)
            load_weights(sp, KV_W)
            sp.wait_ge(key_made, 1)
            sp.dma_start(key_dram.rearrange("u e -> (u e)").rearrange("(p f) -> p f", p=P), krow).then_inc(key_stored, 16)

            def load_x(n, u, i):
                sp.wait_ge(xn_ready, n + 1)
                sp.dma_start(x_in[u], x[bass.ds(P * (n + 2), P), :]).then_inc(x_ld[u], 16)

            over_tiles(sp, load_x, T - 2)
            sp.wait_ge(key_stored, 16)
            finish_phase(sp, 0)

            for u in range(2):
                sp.dma_start(kb[u], key_dram[u:u + 1, :].partition_broadcast(P)).then_inc(kb_in[u], 16)
            with sp.Fori(0, UNITS // 2 - 1) as i:
                for u in range(2):
                    sp.wait_ge(unit_scanned, 2 * i + u + 1)
                    sp.dma_start(kb[u], key_dram[bass.ds(2 * i + u + 2, 1), :].partition_broadcast(P))\
                        .then_inc(kb_in[u], 16)
            finish_phase(sp, 1)

            load_weights(sp, QP_W)
            weights_ready(sp, QP_W)
            sp.dma_start(brow3, b_proj.partition_broadcast(P)).then_inc(rows_in, 16)
            with sp.Fori(0, C) as c:
                for t in range(TC + 1):
                    if t < TC:
                        s, j = y_use[t]
                        sp.wait_ge(xl_used[s], c * y_uses[s] + j + 1)
                        sp.dma_start(xl3[s], xn_dram[bass.ds(c * CW + t * P, P), :]).then_inc(xl_in[s], 16)
                    if t:
                        sp.wait_ge(y_ready, c * TC + t)
                        sp.dma_start(y_dram[bass.ds(c * CW + (t - 1) * P, P), :], y_sb[y_use[t - 1][0]])\
                            .then_inc(y_st[y_use[t - 1][0]], 16)
            sp.wait_ge(y_st[0], 16 * C * y_uses[0])
            sp.wait_ge(y_st[1], 16 * C * y_uses[1])
            finish_phase(sp, 2)

            sp.wait_ge(scattered, 16 * ET)
            for u in range(2):
                sp.dma_start(a_in[u], cells_t[u]).then_inc(L1.a_ld[u], 16)
            for u in range(2):
                sp.dma_start(xl[u], xn_dram[u * P:(u + 1) * P, :]).then_inc(pre_ld[u], 16)

            def load_pre(n, u, i):
                sp.wait_ge(pre_sc, n + 1)
                sp.dma_start(xl[u], xn_dram[bass.ds(P * (n + 2), P), :]).then_inc(pre_ld[u], 16)

            over_tiles(sp, load_pre, T - 2)
            load_weights(sp, G1_W)
            weights_ready(sp, G1_W)
            sp.dma_start(row_a, b1.partition_broadcast(P)).then_inc(rows_in, 16)

            def load_counts(L):
                for u in range(2):
                    sp.dma_start(a_in[u], cells_t[u]).then_inc(L.a_ld[u], 16)

            def next_counts(L, n, u):
                sp.wait_ge(L.alo, n + 1)
                sp.dma_start(a_in[u], cells_t[bass.ds(n + 2, 1)].rearrange("t p f -> (t p) f"))\
                    .then_inc(L.a_ld[u], 16)

            over_tiles(sp, lambda n, u, i: next_counts(L1, n, u), T - 2)
            finish_phase(sp, 3)

            load_counts(L2)
            for c in range(C):
                for i, src in enumerate((hhi_dram, hlo_dram)):
                    sp.dma_start(X[i][:, c * TC:(c + 1) * TC, :],
                                 src[c * CW:(c + 1) * CW, :].rearrange("(t p) d -> p t d", p=P)).then_inc(X_in[c], 16)
            for u in range(2):
                sp.dma_start(xl[u], x[u * P:(u + 1) * P, :]).then_inc(L2.x_ld[u], 16)
                sp.dma_start(yl[u], y_dram[u * P:(u + 1) * P, :]).then_inc(L2.x_ld[u], 16)
            load_weights(sp, G2_W)
            weights_ready(sp, G2_W)
            for dst, src in ((row_a, b2), (row_g, gamma), (row_t, beta)):
                sp.dma_start(dst, src.partition_broadcast(P)).then_inc(rows_in, 16)

            def load_l2(n, u, i):
                next_counts(L2, n, u)
                sp.wait_ge(L2.z_ev, n + 1)
                sp.dma_start(xl[u], x[bass.ds(P * (n + 2), P), :]).then_inc(L2.x_ld[u], 16)
                sp.dma_start(yl[u], y_dram[bass.ds(P * (n + 2), P), :]).then_inc(L2.x_ld[u], 16)

            over_tiles(sp, load_l2, T - 2)
            finish_phase(sp, 4)

            for u in range(2):
                sp.dma_start(fx[u], x2_dram[u * P:(u + 1) * P, :]).then_inc(f_ld[u], 16)
                sp.dma_start(fr[u], x2_dram[u * P:(u + 1) * P, :]).then_inc(fr_ld[u], 16)
            load_weights(sp, FIN_W, FOUT_W)

            def load_f(n, u, i):
                sp.wait_ge(f_norm, n + 1)
                sp.dma_start(fx[u], x2_dram[bass.ds(P * (n + 2), P), :]).then_inc(f_ld[u], 16)
                sp.wait_ge(f_out, n + 1)
                sp.dma_start(fr[u], x2_dram[bass.ds(P * (n + 2), P), :]).then_inc(fr_ld[u], 16)

            over_tiles(sp, load_f, T - 2)

        @block.gpsimd
        def _(pool):
            spacer[pool] = sem("pool_spacer")
            made = Chain(pool, sem("pool_chain"))
            nc.gpsimd.memset(zeros, 0.0).then_inc(zeros_ready, 1)
            made.link(nc.gpsimd.memset(ident, 0.0))
            made.link(nc.gpsimd.affine_select(out=ident, in_=ident, compare_op=ALU.not_equal, fill=1.0, base=0,
                                              pattern=[[-1, P]], channel_multiplier=1))
            made.link(nc.gpsimd.iota(iota, pattern=[[1, P]], base=0, channel_multiplier=0,
                                     allow_small_or_imprecise_dtypes=True))
            made.link(nc.gpsimd.iota(iota8, pattern=[[1, NX]], base=0, channel_multiplier=0,
                                     allow_small_or_imprecise_dtypes=True))
            made.link(nc.gpsimd.memset(valid, 1.0))
            made.link(nc.gpsimd.affine_select(out=valid, in_=valid, compare_op=ALU.is_ge, fill=0.0, base=N - 1,
                                              pattern=[[-P, T]], channel_multiplier=-1))
            made.link(nc.gpsimd.memset(earlier, 1.0))
            for q in range(G):
                made.link(nc.gpsimd.affine_select(out=earlier[:, q, :], in_=earlier[:, q, :], compare_op=ALU.is_ge,
                                                  fill=1.0 + EARLIER, base=-q * P, pattern=[[1, G * P]],
                                                  channel_multiplier=-1))
            made.link(nc.gpsimd.memset(rfa[DH:P, :], -0.5))
            made.link(nc.gpsimd.memset(rfb[0:DH, :], -0.5))
            made.link(nc.gpsimd.memset(ones60, 1.0))
            made.link(nc.gpsimd.memset(epsb, LN_EPS))
            made.link(nc.gpsimd.memset(deg, 0.0))
            pool.wait_ge(consts_in, 32)
            nc.gpsimd.memset(bits, 0.0).then_inc(consts, 1)

            def scatter(b):
                pool.wait_ge(idx_ready, b + 1)
                apart(pool)
                if reused(b):
                    pool.wait_ge(scattered, b * (16 * EPU))
                    apart(pool)
                nc.gpsimd.tensor_copy(idx_b, idx_all[:, bass.ds(b * EPU, EPU)]).then_inc(pool_copied, 1)
                nc.gpsimd.tensor_copy(val_b, val_all[:, bass.ds(b * EPU, EPU)]).then_inc(pool_copied, 1)
                pool.wait_ge(pool_copied, 2 * b + 2)
                apart(pool)
                for j in range(EPU):
                    if j % G == 0 and j:
                        pool.wait_ge(scattered, b * (16 * EPU) + 16 * j)
                        apart(pool)
                    nc.gpsimd.indirect_dma_start(
                        cells, bass.IndirectOffsetOnAxis(ap=idx_b[:, j:j + 1], axis=0), val_b[:, j:j + 1], None,
                        bounds_check=CELLS - 1, oob_is_err=False, compute_op=ALU.add).then_inc(scattered, 16)

            pool.wait_ge(cleared, 16 * T)
            scatter(0)
            with pool.Fori(1, UNITS) as b:
                scatter(b)
            pool.wait_ge(scattered, 16 * ET)
            pool.wait_ge(flag_max, 1)
            nc.gpsimd.partition_all_reduce(flag_f[:, 1:2], flag_f[:, 0:1], P, bass.bass_isa.ReduceOp.max)\
                .then_inc(flag_max, 1)

        @block.scalar
        def _(act):
            spacer[act] = sem("act_spacer")
            act.wait_ge(zeros_ready, 1)
            act.wait_ge(consts, 1)
            act.sem_inc(ev_hi, 2)
            split_hi(act, KV_W)

            def evict_hi(n):
                act.wait_ge(tr_done, n + 3)
                apart(act)
                nc.scalar.copy(xT[0][:, :, bass.ds(n * P, P)], halves6(bank16u_hi(n))).then_inc(ev_hi, 1)

            halves6 = lambda ap: ap[:, 0:D].rearrange("p (k n) -> p k n", k=K)
            slot_of = {}

            def bank16u_hi(n):
                return bank16(2 * slot_of["prev"])

            def ln1(n, u, i):
                act.wait_ge(var_ready, n + 1)
                nc.scalar.activation(bits[:, u, 0:1], bits[:, u, 1:2], ACT.Sqrt).then_inc(sd_ready, 1)
                if reused(n):
                    slot_of["prev"] = 1 - u
                    evict_hi(n - 1)
                act.wait_ge(xn_ready, n + 1)
                act.wait_ge(tr_done, n + 1)
                nc.scalar.copy(xhi[u], xn[u]).then_inc(hi_ready, 1)
                act.dma_start(xn_dram[bass.ds(n * P, P), :], xn[u]).then_inc(xn_st[u], 16)
                act.dma_start(cells_t[bass.ds(n, 1)].rearrange("t p f -> (t p) f"), zeros).then_inc(cleared, 16)

            over_tiles(act, ln1)
            slot_of["prev"] = 0
            evict_hi(T - 1)
            act.wait_ge(xn_st[0], 16 * 13)
            act.wait_ge(xn_st[1], 16 * 12)
            finish_phase(act, 0)

            act.sem_inc(kp_exp, 2)
            act.sem_inc(slot_free[0], 2)
            act.sem_inc(slot_free[1], 2)

            def square_k(c, p):
                act.wait_ge(kk_cp, 2 * (c * PAIRS + p) + 2)
                nc.scalar.activation(kk[p % 2][DH:P, 0, :], kk[p % 2][0:DH, 0, :], ACT.Square).then_inc(kk_sq, 1)
                nc.scalar.activation(kk[p % 2][0:DH, 1, :], kk[p % 2][DH:P, 1, :], ACT.Square).then_inc(kk_sq, 1)

            bank_pair = lambda s: pair[s][:, :, 0:HW]

            act.wait_ge(vals_clear, 1)
            with act.Fori(0, C) as c:
                for t in range(TC):
                    s, j = slot_use[("v", t)]
                    act.wait_ge(slot_full[s], c * uses[s] + j + 1)
                    apart(act)
                    nc.scalar.activation(
                        vals[:, t, :, 0:DH].rearrange("p (a h) d -> p a h d", a=2),
                        wide(s).rearrange("p a (h d) -> p a h d", h=H // 2), ACT.Copy,
                        scale=valid[:, bass.ds(c * TC + t, 1)]).then_inc(slot_free[s], 2)
                square_k(c, 0)
                for p in range(PAIRS):
                    for t in range(TC):
                        q = (p * TC + t) % 2
                        act.wait_ge(kp_full, (c * PAIRS + p) * TC + t + 1)
                        nc.scalar.activation(kp_sb[q], bank(4 + q), ACT.Exp).then_inc(kp_exp, 1)
                        if t == 2 and p + 1 < PAIRS:
                            square_k(c, p + 1)
            act.wait_ge(cleared, 16 * T)
            finish_phase(act, 1)

            split_hi(act, QP_W)
            act.sem_inc(qt_free, 1)
            for s in range(2):
                act.sem_inc(qp_free[s], 1)
                act.sem_inc(xl_used[s], 1)

            def square_q(c, p):
                act.wait_ge(qq_cp, 2 * (c * PAIRS + p) + 2)
                nc.scalar.activation(kk[p % 2][DH:P, 0, :], kk[p % 2][0:DH, 0, :], ACT.Square).then_inc(qq_sq, 1)
                nc.scalar.activation(kk[p % 2][0:DH, 1, :], kk[p % 2][DH:P, 1, :], ACT.Square).then_inc(qq_sq, 1)

            def chunk3(c, more=True):
                for p in range(PAIRS):
                    for g in range(4):
                        s, j = q_use[("q", p, g)]
                        act.wait_ge(qp_full[s], c * q_uses[s] + j + 1)
                        nc.scalar.activation(qp_sb[p % 2][:, g, :].rearrange("p (a b) -> p a b", a=2),
                                             bank_pair(1 + s), ACT.Exp).then_inc(qp_free[s], 1)
                    act.wait_ge(qp_free[0], c * q_uses[0] + 2 * p + 3)
                    act.wait_ge(qp_free[1], c * q_uses[1] + 2 * p + 3)
                    act.sem_inc(qp_exp, 1)
                    if p + 1 < PAIRS:
                        square_q(c, p + 1)

                def high(t):
                    act.wait_ge(attn_done, (c + 1) * PAIRS)
                    act.wait_ge(atr_full, c * TC + t + 1)
                    nc.scalar.copy(ahi[t % 2], attn[:, t, :]).then_inc(ahi_ready, 1)

                high(0)
                high(1)
                for t in range(TC):
                    act.wait_ge(atr_full, c * TC + t + 3)
                    nc.scalar.copy(aT[0][t % 2], bank16(6)[:, 0:D]).then_inc(aT_hi, 1)
                    if t + 2 < TC:
                        high(t + 2)
                    if t == 1 and more:
                        square_q(c + 1, 0)

            square_q(0, 0)
            with act.Fori(0, C - 1) as c:
                chunk3(c)
            chunk3(C - 1, False)
            act.wait_ge(sq_asked, 1)
            nc.scalar.activation(t25[:, 0, :], deg[:, 0:T], ACT.Sqrt).then_inc(sq_done, 1)
            nc.scalar.activation(t25[:, 1, :], mvy[:, :, 1], ACT.Sqrt).then_inc(sq_done, 1)
            act.wait_ge(sq_done, 2)
            finish_phase(act, 2)


            def pre(n, u, i):
                act.wait_ge(pre_sc, n + 1)
                apart(act)
                nc.scalar.copy(X[0][:, bass.ds(n, 1), :].rearrange("p a b -> p (a b)"), zt[u]).then_inc(pre_hi, 1)

            def layer(L, first, seg):
                def counts(n, u, i):
                    act.wait_ge(L.a_ld[u], 16 * i + 16)
                    act.wait_ge(L.g_full, n + 1)
                    nc.scalar.copy(a_hi[u].rearrange("p a b -> p (a b)"), a_in[u]).then_inc(L.ahi, 1)

                def split_g(n, u):
                    act.wait_ge(L.g_full, n + 3)
                    act.wait_ge(L.tr, n + 1)
                    nc.scalar.copy(halves(ghi[u]), wide(u)).then_inc(L.ghi, 1)

                def evict(n, u):
                    act.wait_ge(L.tr, n + 3)
                    nc.scalar.copy(gT[0][u], bank16(4)[:, 0:D]).then_inc(L.gT_hi, 1)

                def finish1(n, u, i):
                    act.wait_ge(L.z_ev, n + 1)
                    apart(act)
                    nc.scalar.activation(zr[u], zt[u], ACT.Relu, scale=dinv[:, bass.ds(n, 1)]).then_inc(L.relu, 1)
                    act.wait_ge(L.relu, n + 3)
                    if reused(i):
                        act.wait_ge(L.st[u], 32 * i)
                    nc.scalar.copy(zhi[u], zr[u]).then_inc(L.zhi, 1)
                    act.wait_ge(L.zhi, n + 1)
                    act.dma_start(hhi_dram[bass.ds(n * P, P), :], zhi[u]).then_inc(L.st[u], 16)
                    act.wait_ge(L.zlo, n + 1)
                    act.dma_start(hlo_dram[bass.ds(n * P, P), :], zlo[u]).then_inc(L.st[u], 16)

                def finish2(n, u, i):
                    act.wait_ge(L.z_ev, n + 1)
                    act.dma_start(x2_dram[bass.ds(n * P, P), :], zt[u]).then_inc(L.st[u], 16)

                def body(n, u, i, more=True):
                    if more:
                        counts(n + 1, 1 - u, i if u == 0 else i + 1)
                    if reused(n):
                        evict(n - 1, 1 - u)
                    split_g(n, u)
                    if reused(n):
                        (finish1 if first else finish2)(n - 1, 1 - u, i if u == 1 else i - 1)

                act.sem_inc(L.relu, 2)
                counts(0, 0, 0)
                counts(1, 1, 0)
                if first:
                    over_tiles(act, pre)
                split_hi(act, seg)
                body(0, 0, 0, False)
                body(1, 1, 0)
                body(2, 0, 1)
                with act.Fori(0, (T - 5) // 2) as i:
                    body(2 * i + 3, 1, i + 1)
                    body(2 * i + 4, 0, i + 2)
                body(T - 2, 1, T // 2 - 1)
                body(T - 1, 0, T // 2, False)
                evict(T - 1, 0)
                (finish1 if first else finish2)(T - 1, 0, (T - 1) // 2)
                act.wait_ge(L.st[0], (32 if first else 16) * 13)
                act.wait_ge(L.st[1], (32 if first else 16) * 12)

            layer(L1, True, G1_W)
            finish_phase(act, 3)
            layer(L2, False, G2_W)
            act.wait_ge(L2.done, 1)
            nc.scalar.activation(t25[:, 0, :], mv2[:, :, 1], ACT.Sqrt).then_inc(sq_done, 1)
            act.wait_ge(sq_done, 3)
            finish_phase(act, 4)

            def f_high(n, u):
                act.wait_ge(f_norm, n + 1)
                act.wait_ge(f_tr, n + 1)
                nc.scalar.copy(fhi[u], fn[u]).then_inc(f_hi, 1)

            def f_evict(n, u):
                act.wait_ge(f_tr, n + 3)
                nc.scalar.copy(fT[0][u], bank16(0)[:, 0:D]).then_inc(fT_hi, 1)

            def silu(n):
                act.wait_ge(f_hsel, n + 1)
                nc.scalar.activation(hact, hsel, ACT.Silu).then_inc(f_act, 1)
                act.wait_ge(f_act, n + 1)
                nc.scalar.copy(act_hi, hact).then_inc(f_ahi, 1)

            def m_evict(n, u):
                act.wait_ge(f_mtr, n + 1)
                nc.scalar.copy(mT[0][u], bank16(0)).then_inc(mT_hi, 1)

            def store(n, u):
                act.wait_ge(f_out, n + 1)
                act.dma_start(out[bass.ds(n * P, P), :], fo[u]).then_inc(f_st[u], 16)

            f_high(0, 0)
            split_hi(act, FIN_W)
            f_evict(0, 0)
            split_hi(act, FOUT_W)

            def experts(n, u, i):
                f_high(n + 1, 1 - u)
                f_evict(n + 1, 1 - u)
                silu(n)
                m_evict(n, u)
                if reused(n):
                    store(n - 1, 1 - u)

            over_tiles(act, experts, T - 2)
            for n in (T - 2, T - 1):
                u = n % 2
                if n + 1 < T:
                    f_high(n + 1, 1 - u)
                    f_evict(n + 1, 1 - u)
                silu(n)
                m_evict(n, u)
                store(n - 1, 1 - u)
            store(T - 1, 0)
            act.wait_ge(f_st[0], 16 * 13)
            act.wait_ge(f_st[1], 16 * 12)

        @block.vector
        def _(dve):
            spacer[dve] = sem("dve_spacer")
            e = Chain(dve, dve_done, links(16))
            dve.wait_ge(edges_in, 64)
            for r, (row, key) in enumerate(((0, krow), (4, kcol))):
                s_lo, s_hi, d_lo, d_hi = eint[row + 1], eint[row], eint[row + 3], eint[row + 2]
                for lo, hi in ((s_lo, s_hi), (d_lo, d_hi)):
                    e.link(nc.vector.tensor_scalar(lo, hi, P - 1, None, ALU.bitwise_and))
                    e.link(nc.vector.tensor_scalar(hi, hi, 7, None, ALU.logical_shift_right))
                e.link(nc.vector.scalar_tensor_tensor(ktmp, d_hi, float(P * NP), d_lo, ALU.mult, ALU.add))
                e.link(nc.vector.scalar_tensor_tensor(ktmp, s_lo, float(NP), ktmp, ALU.mult, ALU.add))
                ins = nc.vector.scalar_tensor_tensor(key, s_hi, float(P), ktmp, ALU.mult, ALU.add)
                e.link(ins)
                if r == 0:
                    dve.sem_inc(key_made, 1)
            e.link(nc.vector.tensor_scalar(dst_lo16, d_lo, 0.0, None, ALU.add))
            e.link(nc.vector.tensor_scalar(dst_hi16, d_hi, 0.0, None, ALU.add))
            dve.sem_inc(ev_lo, 2)
            split_lo(dve, KV_W)
            dve.wait_ge(consts, 1)

            def newton(chain, r, v, sd, t):
                chain.link(nc.vector.reciprocal(r, sd))
                chain.link(nc.vector.tensor_tensor(t, r, r, ALU.mult))
                chain.link(nc.vector.tensor_tensor(t, t, v, ALU.mult))
                chain.link(nc.vector.tensor_scalar(t, t, -0.5, 1.5, ALU.mult, ALU.add))
                chain.link(nc.vector.tensor_tensor(r, r, t, ALU.mult))

            halves6 = lambda ap: ap[:, 0:D].rearrange("p (k n) -> p k n", k=K)
            LN1_LINKS = 8
            ln1_base = links(LN1_LINKS, T)

            def evict_lo(n, u):
                dve.wait_ge(tr_done, n + 3)
                apart(dve)
                nc.vector.tensor_copy(xT[1][:, :, bass.ds(n * P, P)], halves6(bank16(2 * u + 1))).then_inc(ev_lo, 1)

            def ln1(n, u, i):
                ch = Chain(dve, dve_done, n * LN1_LINKS + ln1_base)
                dve.wait_ge(x_ld[u], 16 * i + 16)
                nc.vector.bn_stats(bst[:, u, 0:6], x_in[u][:, 0:HD])
                ch.link(nc.vector.bn_stats(bst[:, u, 6:12], x_in[u][:, HD:D]))
                apart(dve)
                ch.link(nc.vector.bn_aggr(bits[:, u, 4:6], bst[:, u, :]))
                nc.vector.tensor_scalar(bits[:, u, 1:2], bits[:, u, 5:6], LN_EPS, None, ALU.add).then_inc(var_ready, 1)
                if reused(n):
                    evict_lo(n - 1, 1 - u)
                dve.wait_ge(sd_ready, n + 1)
                dve.wait_ge(var_ready, n + 1)
                newton(ch, bits[:, u, 2:3], bits[:, u, 1:2], bits[:, u, 0:1], bits[:, u, 3:4])
                if reused(i):
                    dve.wait_ge(xn_st[u], 16 * i)
                ch.link(nc.vector.tensor_scalar(xn[u], x_in[u], bits[:, u, 4:5], bits[:, u, 2:3],
                                                ALU.subtract, ALU.mult))
                assert ch.n == LN1_LINKS
                dve.sem_inc(xn_ready, 1)
                dve.wait_ge(hi_ready, n + 1)
                nc.vector.tensor_tensor(xlo[u], xn[u], xhi[u], ALU.subtract).then_inc(lo_ready, 1)

            over_tiles(dve, ln1)
            evict_lo(T - 1, 0)
            finish_phase(dve, 0)

            dve.sem_inc(scan_done, 2)
            dve.sem_inc(kv_free, 1)
            dve.sem_inc(deg_free, 1)
            ch = Chain(dve, dve_done, links(2))
            ch.link(nc.vector.memset(kv, 0.0))
            ch.link(nc.vector.memset(vals, 0.0))
            dve.sem_inc(vals_clear, 1)
            bank_pair = lambda s: pair[s][:, :, 0:HW]
            UNIT_LINKS = 3
            unit_base = links(UNIT_LINKS, UNITS)

            def copy_k(c, p):
                s, j = slot_use[("k", p)]
                dve.wait_ge(slot_full[s], c * uses[s] + j + 1)
                src = bank_pair(s)
                nc.vector.tensor_copy(kk[p % 2][0:DH, 0, :].rearrange("p (a b) -> p a b", a=2), src[0:DH])\
                    .then_inc(kk_cp, 1)
                nc.vector.tensor_copy(kk[p % 2][DH:P, 1, :].rearrange("p (a b) -> p a b", a=2), src[DH:P])\
                    .then_inc(kk_cp, 1)
                dve.wait_ge(kk_cp, 2 * (c * PAIRS + p) + 2)
                dve.sem_inc(slot_free[s], 2)

            def scan(c, p):
                m = c * PAIRS + p
                dve.wait_ge(kb_in[p % 2], 16 * (c * (PAIRS // 2) + p // 2 + 1))
                for j in range(EPU):
                    dve.wait_ge(scan_done, m * EPU + (j + 1))
                    nc.vector.scalar_tensor_tensor(
                        out=junk[j % 2], in0=kb[p % 2][:, (j // G) * G * P:(j // G + 1) * G * P],
                        scalar=kcol[:, bass.ds(m * EPU + j, 1)], in1=earlier[:, j % G, :], op0=ALU.is_equal,
                        op1=ALU.mult, accum_out=sums[:, j:j + 1]).then_inc(scan_done, 1)
                dve.wait_ge(scan_done, m * EPU + (EPU + 2))
                dve.sem_inc(unit_scanned, 1)
                cu = Chain(dve, dve_done, m * UNIT_LINKS + unit_base)
                cu.link(nc.vector.tensor_scalar(skip, sums, EARLIER, FAR, ALU.is_ge, ALU.mult))
                cu.link(nc.vector.tensor_tensor(idx_all[:, bass.ds(m * EPU, EPU)], kcol[:, bass.ds(m * EPU, EPU)],
                                                skip, ALU.add))
                cu.link(nc.vector.tensor_scalar(val_all[:, bass.ds(m * EPU, EPU)], sums, 0.0, None, ALU.add))
                dve.sem_inc(idx_ready, 1)
                iota_b = iota.rearrange("p (o n) -> p o n", o=1).to_broadcast([P, EPU, P])
                nc.vector.tensor_tensor(oh_lo, iota_b, dst_lo16[:, bass.ds(m * EPU, EPU)].rearrange(
                    "p (j o) -> p j o", o=1).to_broadcast([P, EPU, P]), ALU.is_equal).then_inc(oh_ready, 1)
                iota_h = iota[:, 0:26].rearrange("p (o n) -> p o n", o=1).to_broadcast([P, EPU, 26])
                nc.vector.tensor_tensor(oh_hi, iota_h, dst_hi16[:, bass.ds(m * EPU, EPU)].rearrange(
                    "p (j o) -> p j o", o=1).to_broadcast([P, EPU, 26]), ALU.is_equal).then_inc(oh_ready, 1)

            def add_kv(c, p):
                m = c * PAIRS + p
                dve.wait_ge(kv_full, m + 1)
                dst = kv[:, p, :, :].rearrange("p a b -> p (a b)")
                nc.vector.tensor_tensor(dst, dst, bank(6)[:, 0:4 * VW], ALU.add).then_inc(kv_free, 1)
                dve.wait_ge(deg_full, m + 1)
                dve.wait_ge(deg_free, m + 1)
                nc.vector.tensor_tensor(deg, deg, bank(7)[:, 0:26], ALU.add).then_inc(deg_free, 1)

            with dve.Fori(0, C) as c:
                dve.wait_ge(slot_full[0], c * uses[0] + 1)
                apart(dve)
                nc.vector.tensor_tensor(
                    vals[:, :, :, DH], valid[:, bass.ds(c * TC, TC)].rearrange("p (t o) -> p t o", o=1)
                    .to_broadcast([P, TC, H]), ones60.rearrange("p (t h) -> p t h", t=TC), ALU.mult)\
                    .then_inc(vone_ready, 1)
                copy_k(c, 0)
                for p in range(PAIRS):
                    scan(c, p)
                    if p + 1 < PAIRS:
                        copy_k(c, p + 1)
                    add_kv(c, p)
            finish_phase(dve, 1)

            split_lo(dve, QP_W)
            nc.vector.tensor_scalar(kv, kv, 1.0 / M, None, ALU.mult).then_inc(kv_scaled, 1)
            nc.vector.tensor_reduce(flag_f[:, 0:1], deg[:, 0:T], AXX, ALU.max).then_inc(flag_max, 1)
            dve.wait_ge(rows_in, 16)

            def copy_q(c, p):
                dve.wait_ge(qt_full, c * PAIRS + p + 1)
                src = bank_pair(0)
                nc.vector.tensor_copy(kk[p % 2][0:DH, 0, :].rearrange("p (a b) -> p a b", a=2), src[0:DH])\
                    .then_inc(qq_cp, 1)
                nc.vector.tensor_copy(kk[p % 2][DH:P, 1, :].rearrange("p (a b) -> p a b", a=2), src[DH:P])\
                    .then_inc(qq_cp, 1)
                dve.wait_ge(qq_cp, 2 * (c * PAIRS + p) + 2)
                dve.sem_inc(qt_free, 1)

            o_parts = [(0, 3, pair[3][:, 0, 0:3 * 2 * VW].rearrange("p (t h e) -> p t h e", t=3, h=2)),
                       (3, 5, pair[3][:, 1, 0:2 * 2 * VW].rearrange("p (t h e) -> p t h e", t=2, h=2))]

            def normalise(c, p):
                m = c * PAIRS + p
                cn = Chain(dve, dve_done, c * (q_links + y_links) + (q_base + 4 * p))
                dve.wait_ge(o_full, m + 1)
                nc.vector.tensor_scalar(rden[:, 0:3, :], o_parts[0][2][:, :, :, DH], 1e-6, None, ALU.add)
                cn.link(nc.vector.tensor_scalar(rden[:, 3:5, :], o_parts[1][2][:, :, :, DH], 1e-6, None, ALU.add))
                cn.link(nc.vector.reciprocal(rden, rden))
                for a, b, o in o_parts:
                    cn.link(nc.vector.tensor_tensor(
                        attn[:, a:b, p * P:(p + 1) * P].rearrange("p t (h e) -> p t h e", h=2), o[:, :, :, 0:DH],
                        rden[:, a:b, :].rearrange("p t (h o) -> p t h o", o=1).to_broadcast([P, b - a, 2, DH]),
                        ALU.mult))
                dve.sem_inc(attn_done, 1)

            q_links, y_links = 4 * PAIRS, 3 * TC
            q_base = links(q_links + y_links, C)

            def chunk3(c, more=True):
                for p in range(PAIRS):
                    if p + 1 < PAIRS:
                        copy_q(c, p + 1)
                    normalise(c, p)

                def low(t):
                    dve.wait_ge(ahi_ready, c * TC + t + 1)
                    nc.vector.tensor_tensor(alo[t % 2], attn[:, t, :], ahi[t % 2], ALU.subtract).then_inc(alo_ready, 1)

                def rows(t):
                    s, j = q_use[("y", t)]
                    ys, yj = y_use[t]
                    cr = Chain(dve, dve_done, c * (q_links + y_links) + (q_base + q_links + 3 * t))
                    dve.wait_ge(qp_full[s], c * q_uses[s] + j + 1)
                    dve.wait_ge(xl_in[ys], 16 * (c * y_uses[ys] + yj + 1))
                    if reused(c) or yj:
                        dve.wait_ge(y_st[ys], 16 * (c * y_uses[ys] + yj))
                    nc.vector.tensor_tensor(halves(y_sb[ys]), wide(1 + s), halves(xl3[ys]), ALU.add)\
                        .then_inc(xl_used[ys], 1)
                    dve.wait_ge(xl_used[ys], c * y_uses[ys] + yj + 2)
                    dve.sem_inc(qp_free[s], 1)
                    cr.link(nc.vector.tensor_tensor(y_sb[ys], y_sb[ys], brow3, ALU.add))
                    dve.sem_inc(y_ready, 1)
                    nc.vector.bn_stats(bst[:, 0, 0:6], y_sb[ys][:, 0:HD])
                    cr.link(nc.vector.bn_stats(bst[:, 0, 6:12], y_sb[ys][:, HD:D]))
                    apart(dve)
                    cr.link(nc.vector.bn_aggr(mvt[:, t, :], bst[:, 0, :]))

                low(0)
                low(1)
                for t in range(TC):
                    dve.wait_ge(atr_full, c * TC + t + 3)
                    nc.vector.tensor_copy(aT[1][t % 2], bank16(7)[:, 0:D]).then_inc(aT_lo, 1)
                    if t + 2 < TC:
                        low(t + 2)
                    if t == 0 and more:
                        copy_q(c + 1, 0)
                    if t:
                        rows(t - 1)
                rows(TC - 1)
                nc.vector.tensor_scalar(mvy[:, bass.ds(c * TC, TC), :], mvt, 0.0, None, ALU.add).then_inc(mvy_done, 1)
                dve.wait_ge(mvy_done, c + 1)

            copy_q(0, 0)
            chunk3(0)
            with dve.Fori(1, C - 1) as c:
                chunk3(c)
            chunk3(C - 1, False)
            cs = Chain(dve, dve_done, links(12))
            cs.link(nc.vector.tensor_scalar(mvy[:, :, 1], mvy[:, :, 1], LN_EPS, None, ALU.add))
            dve.sem_inc(sq_asked, 1)
            dve.wait_ge(sq_done, 2)
            newton(cs, dinv, deg[:, 0:T], t25[:, 0, :], t25[:, 2, :])
            newton(cs, ry, mvy[:, :, 1], t25[:, 1, :], t25[:, 2, :])
            dve.wait_ge(flag_max, 2)
            cs.link(nc.vector.tensor_scalar(flag_i, flag_f[:, 1:2].to_broadcast([P, 2]), COUNT_EXACT, None, ALU.is_gt))
            dve.sem_inc(flag_ready, 1)
            finish_phase(dve, 2)

            def pre_low(n, u):
                dve.wait_ge(pre_hi, n + 1)
                nc.vector.tensor_tensor(X[1][:, bass.ds(n, 1), :].rearrange("p a b -> p (a b)"), zt[u],
                                        X[0][:, bass.ds(n, 1), :].rearrange("p a b -> p (a b)"), ALU.subtract)\
                    .then_inc(pre_lo, 1)

            def pre(n, u, i):
                dve.wait_ge(pre_ld[u], 16 * i + 16)
                if reused(i):
                    dve.wait_ge(pre_lo, n - 1)
                    apart(dve)
                nc.vector.tensor_scalar(zt[u], xl[u], dinv[:, bass.ds(n, 1)], None, ALU.mult).then_inc(pre_sc, 1)
                if reused(n):
                    pre_low(n - 1, 1 - u)

            def layer(L, first, seg):

                def counts(n, u):
                    dve.wait_ge(L.ahi, n + 1)
                    nc.vector.tensor_tensor(a_lo[u].rearrange("p a b -> p (a b)"), a_in[u],
                                            a_hi[u].rearrange("p a b -> p (a b)"), ALU.subtract).then_inc(L.alo, 1)

                def split_g(n, u):
                    dve.wait_ge(L.ghi, n + 1)
                    nc.vector.tensor_tensor(halves(glo[u]), wide(u), halves(ghi[u]), ALU.subtract).then_inc(L.glo, 1)

                def evict(n, u):
                    dve.wait_ge(L.tr, n + 3)
                    nc.vector.tensor_copy(gT[1][u], bank16(5)[:, 0:D]).then_inc(L.gT_lo, 1)

                def finish1(n, u, i):
                    dve.wait_ge(L.z_full, n + 1)
                    dve.wait_ge(L.relu, n + 1)
                    nc.vector.scalar_tensor_tensor(halves(zt[u]), wide(3), dinv[:, bass.ds(n, 1)], halves(row_a),
                                                   ALU.mult, ALU.add).then_inc(L.z_ev, 1)
                    dve.wait_ge(L.zhi, n + 1)
                    nc.vector.tensor_tensor(zlo[u], zr[u], zhi[u], ALU.subtract).then_inc(L.zlo, 1)

                LINKS = 7
                row_base = 0 if first else links(1)
                l2_base = 0 if first else links(LINKS, T)

                def finish2(n, u, i):
                    cc = Chain(dve, dve_done, n * LINKS + l2_base)
                    dve.wait_ge(L.x_ld[u], 32 * i + 32)
                    cc.link(nc.vector.tensor_scalar(yl[u], yl[u], mvy[:, bass.ds(n, 1), 0], ry[:, bass.ds(n, 1)],
                                                    ALU.subtract, ALU.mult))
                    cc.link(nc.vector.tensor_tensor(yl[u], yl[u], row_g, ALU.mult))
                    cc.link(nc.vector.tensor_tensor(xl[u], xl[u], row_a, ALU.add))
                    cc.link(nc.vector.tensor_tensor(xl[u], xl[u], yl[u], ALU.add))
                    dve.wait_ge(L.z_full, n + 1)
                    if reused(i):
                        dve.wait_ge(L.st[u], 16 * i)
                    cc.link(nc.vector.scalar_tensor_tensor(halves(zt[u]), wide(3), dinv[:, bass.ds(n, 1)],
                                                           halves(xl[u]), ALU.mult, ALU.add))
                    dve.sem_inc(L.z_ev, 1)
                    nc.vector.bn_stats(bst[:, u, 0:6], zt[u][:, 0:HD])
                    cc.link(nc.vector.bn_stats(bst[:, u, 6:12], zt[u][:, HD:D]))
                    apart(dve)
                    cc.link(nc.vector.bn_aggr(mvt[:, u, :], bst[:, u, :]))
                    nc.vector.tensor_scalar(mv2[:, bass.ds(n, 1), :].rearrange("p a b -> p (a b)"), mvt[:, u, :],
                                            0.0, None, ALU.add).then_inc(L.zlo, 1)

                def body(n, u, i, more=True):
                    if more:
                        counts(n + 1, 1 - u)
                    if reused(n):
                        evict(n - 1, 1 - u)
                    split_g(n, u)
                    if reused(n):
                        (finish1 if first else finish2)(n - 1, 1 - u, i if u == 1 else i - 1)

                counts(0, 0)
                counts(1, 1)
                if first:
                    over_tiles(dve, pre)
                    pre_low(T - 1, 0)
                split_lo(dve, seg)
                if first:
                    dve.wait_ge(rows_in, 32)
                else:
                    dve.wait_ge(rows_in, 80)
                    cb = Chain(dve, dve_done, row_base)
                    cb.link(nc.vector.tensor_tensor(row_a, row_a, row_t, ALU.add))
                body(0, 0, 0, False)
                body(1, 1, 0)
                body(2, 0, 1)
                with dve.Fori(0, (T - 5) // 2) as i:
                    body(2 * i + 3, 1, i + 1)
                    body(2 * i + 4, 0, i + 2)
                body(T - 2, 1, T // 2 - 1)
                body(T - 1, 0, T // 2, False)
                evict(T - 1, 0)
                (finish1 if first else finish2)(T - 1, 0, (T - 1) // 2)

            layer(L1, True, G1_W)
            finish_phase(dve, 3)
            layer(L2, False, G2_W)
            dve.wait_ge(L2.zlo, T)
            cb = Chain(dve, dve_done, links(6))
            cb.link(nc.vector.tensor_scalar(mv2[:, :, 1], mv2[:, :, 1], LN_EPS, None, ALU.add))
            dve.sem_inc(L2.done, 1)
            dve.wait_ge(sq_done, 3)
            newton(cb, r2, mv2[:, :, 1], t25[:, 0, :], t25[:, 2, :])
            finish_phase(dve, 4)

            FL = 12

            def f_low(n, u, i):
                dve.wait_ge(f_ld[u], 16 * i + 16)
                nc.vector.tensor_scalar(fn[u], fx[u], mv2[:, bass.ds(n, 1), 0], r2[:, bass.ds(n, 1)],
                                        ALU.subtract, ALU.mult).then_inc(f_norm, 1)
                dve.wait_ge(f_hi, n + 1)
                nc.vector.tensor_tensor(flo[u], fn[u], fhi[u], ALU.subtract).then_inc(f_lo, 1)

            def f_evict(n, u):
                dve.wait_ge(f_tr, n + 3)
                nc.vector.tensor_copy(fT[1][u], bank16(1)[:, 0:D]).then_inc(fT_lo, 1)

            f_base = links(FL, T)

            def select(n, u):
                cf = Chain(dve, dve_done, n * FL + f_base)
                dve.wait_ge(f_h, n + 1)
                cf.link(nc.vector.tensor_reduce(nmax[:, 0:1], bank(4)[:, 384:384 + NX], AXX, ALU.max))
                cf.link(nc.vector.tensor_scalar(lg, bank(4)[:, 384:384 + NX], nmax[:, 0:1], -104.0,
                                                ALU.subtract, ALU.max))
                apart(dve)
                cf.link(nc.vector.max(top, lg))
                apart(dve)
                cf.link(nc.vector.max_index(topi, top, lg))
                cf.link(nc.vector.tensor_copy(topf, topi))
                cf.link(nc.vector.tensor_tensor(esel[:, 0:1], topf[:, 0:1], topf[:, 1:2], ALU.max))
                cf.link(nc.vector.tensor_scalar(mask, iota8, esel[:, 0:1], None, ALU.is_equal))
                nc.vector.tensor_scalar(mask16, iota8, esel[:, 0:1], None, ALU.is_equal)
                m3 = mask.rearrange("p (e o) -> p e o", o=1)
                for b in range(2):
                    ins = nc.vector.tensor_tensor(
                        hsel_all[:, 4 * b:4 * b + 4, :], bank(2 + b).rearrange("p (e i) -> p e i", e=4),
                        m3[:, 4 * b:4 * b + 4].to_broadcast([P, 4, NI]), ALU.mult)
                cf.link(ins)
                nc.vector.tensor_reduce(hsel, hsel_all.rearrange("p e i -> p i e"), AXX, ALU.add).then_inc(f_hsel, 1)
                dve.wait_ge(f_ahi, n + 1)
                cf.link(nc.vector.tensor_tensor(act_lo, hact, act_hi, ALU.subtract))
                k3 = mask16.rearrange("p (e o) -> p e o", o=1).to_broadcast([P, NX, NI])
                for part, dst in ((act_hi, m_hi), (act_lo, m_lo)):
                    ins = nc.vector.tensor_tensor(
                        dst, part.rearrange("p (o i) -> p o i", o=1).to_broadcast([P, NX, NI]), k3, ALU.mult)
                    cf.link(ins)
                dve.sem_inc(f_mask, 1)
                cf.link(nc.vector.tensor_scalar(topf[:, 0:1], topf[:, 0:1], 0.0, None, ALU.add))
                assert cf.n == FL

            def m_evict(n, u):
                dve.wait_ge(f_mtr, n + 1)
                nc.vector.tensor_copy(mT[1][u], bank16(1)).then_inc(mT_lo, 1)

            def finish(n, u, i):
                dve.wait_ge(f_y, n + 1)
                dve.wait_ge(fr_ld[u], 16 * i + 16)
                if reused(i):
                    dve.wait_ge(f_st[u], 16 * i)
                nc.vector.tensor_tensor(halves(fo[u]), wide(3), halves(fr[u]), ALU.add).then_inc(f_out, 1)

            f_low(0, 0, 0)
            split_lo(dve, FIN_W)
            f_evict(0, 0)
            split_lo(dve, FOUT_W)

            def experts(n, u, i):
                f_low(n + 1, 1 - u, i if u == 0 else i + 1)
                f_evict(n + 1, 1 - u)
                select(n, u)
                if reused(n):
                    finish(n - 1, 1 - u, i if u == 1 else i - 1)
                m_evict(n, u)

            over_tiles(dve, experts, T - 2)
            for n in (T - 2, T - 1):
                u = n % 2
                if n + 1 < T:
                    f_low(n + 1, 1 - u, (n + 1) // 2)
                    f_evict(n + 1, 1 - u)
                select(n, u)
                finish(n - 1, 1 - u, (n - 1) // 2)
                m_evict(n, u)
            finish(T - 1, 0, (T - 1) // 2)

        @block.tensor
        def _(pe):
            spacer[pe] = sem("pe_spacer")
            pe.wait_ge(consts, 1)
            pe.sem_inc(tr_done, 2)

            def turn(dst_hi, dst_lo, hi, lo, cols=K):
                for dst, part in ((dst_hi, hi), (dst_lo, lo)):
                    for k in range(cols):
                        ins = nc.tensor.transpose(dst[:, k * P:(k + 1) * P], part[:, k * P:(k + 1) * P], ident)
                return ins

            def tr1(n, u, i):
                pe.wait_ge(lo_ready, n + 1)
                pe.wait_ge(ev_hi, n + 1)
                pe.wait_ge(ev_lo, n + 1)
                turn(bank16(2 * u), bank16(2 * u + 1), xhi[u], xlo[u]).then_inc(tr_done, 1)

            over_tiles(pe, tr1)
            finish_phase(pe, 0)

            def node_cols(c, t):
                return lambda k, part: xT[part][:, k, bass.ds(c * CW + t * P, P)]

            def chunk_cols(c):
                return lambda k, part, half: xT[part][:, k, bass.ds(c * CW + half * HW, HW)]

            def k_up(c, p):
                s, j = slot_use[("k", p)]
                pe.wait_ge(slot_free[s], 2 * (c * uses[s] + j) + 2)
                apart(pe)
                for k in range(K):
                    ins = mm_split(bank_halves(s, HW), lambda k, a: kv_w(k, a)[:, p * P:(p + 1) * P],
                                   chunk_cols(c), k, k == 0, k == K - 1)
                ins.then_inc(slot_full[s], 1)

            def k_features(c, p, t):
                n = p * TC + t
                if t == 0:
                    pe.wait_ge(kk_cp, 2 * (c * PAIRS + p) + 2)
                    pe.wait_ge(kk_sq, 2 * (c * PAIRS + p) + 2)
                pe.wait_ge(kp_exp, c * (PAIRS * TC) + n + 1)
                for h in range(2):
                    ins = nc.tensor.matmul(bank(4 + n % 2)[:, h * M:(h + 1) * M],
                                           kk[p % 2][:, h, t * P:(t + 1) * P], (rfa, rfb)[h], start=True, stop=True)
                ins.then_inc(kp_full, 1)

            def k_sums(c, p, t):
                n = p * TC + t
                if t == 0:
                    pe.wait_ge(kv_free, c * PAIRS + p + 1)
                pe.wait_ge(kp_exp, c * (PAIRS * TC) + n + 3)
                for g in range(4):
                    h, half = g // 2, g % 2
                    ins = nc.tensor.matmul(bank(6)[:, g * VW:(g + 1) * VW],
                                           kp_sb[n % 2][:, h * M + half * P:h * M + (half + 1) * P],
                                           vals[:, t, 2 * p + h, :], start=(t == 0 and g == 0), stop=(t == TC - 1),
                                           skip_group_check=True)
                if t == TC - 1:
                    ins.then_inc(kv_full, 1)

            def degrees(c, p):
                m = c * PAIRS + p
                pe.wait_ge(oh_ready, 2 * m + 2)
                pe.wait_ge(deg_free, m + 1)
                for j in range(EPU):
                    ins = nc.tensor.matmul(bank(7)[:, 0:26], oh_lo[:, j, :], oh_hi[:, j, :], start=(j == 0),
                                           stop=(j == EPU - 1))
                ins.then_inc(deg_full, 1)

            weights_ready(pe, KV_W)
            with pe.Fori(0, C) as c:
                for t in range(TC):
                    s, j = slot_use[("v", t)]
                    pe.wait_ge(slot_free[s], 2 * (c * uses[s] + j) + 2)
                    apart(pe)
                    for k in range(K):
                        ins = mm_split(bank_halves(s, HD), node_cols(c, t),
                                       lambda k, b, half: kv_w(k, b)[:, D + half * HD:D + (half + 1) * HD],
                                       k, k == 0, k == K - 1)
                    ins.then_inc(slot_full[s], 1)
                k_up(c, 0)
                pe.wait_ge(vone_ready, c + 1)
                for p in range(PAIRS):
                    k_features(c, p, 0)
                    k_features(c, p, 1)
                    if p + 1 < PAIRS:
                        k_up(c, p + 1)
                    if p == 0:
                        pe.wait_ge(slot_free[0], 2 * (c * uses[0]) + 8)
                        pe.wait_ge(slot_free[1], 2 * (c * uses[1]) + 6)
                    for t in range(TC):
                        k_sums(c, p, t)
                        if t + 2 < TC:
                            k_features(c, p, t + 2)
                    degrees(c, p)
            finish_phase(pe, 1)

            pe.sem_inc(atr_full, 2)
            weights_ready(pe, QP_W)
            pe.wait_ge(kv_scaled, 1)

            def q_up(c, p):
                pe.wait_ge(qt_free, c * PAIRS + p + 1)
                apart(pe)
                for k in range(K):
                    ins = mm_split(bank_halves(0, HW), lambda k, a: q_w(k, a)[:, p * P:(p + 1) * P],
                                   chunk_cols(c), k, k == 0, k == K - 1)
                ins.then_inc(qt_full, 1)

            def chunk3(c, more=True):
                for p in range(PAIRS):
                    m = c * PAIRS + p
                    pe.wait_ge(qq_cp, 2 * m + 2)
                    pe.wait_ge(qq_sq, 2 * m + 2)
                    for g in range(4):
                        h, half = g // 2, g % 2
                        s, j = q_use[("q", p, g)]
                        pe.wait_ge(qp_free[s], c * q_uses[s] + j + 1)
                        for b in range(2):
                            ins = nc.tensor.matmul(pair[1 + s][:, b, 0:HW], (rfa, rfb)[h][:, half * P:(half + 1) * P],
                                                   kk[p % 2][:, h, b * HW:(b + 1) * HW], start=True, stop=True)
                        ins.then_inc(qp_full[s], 1)
                    if p + 1 < PAIRS:
                        q_up(c, p + 1)
                    pe.wait_ge(qp_exp, m + 1)
                    if p:
                        pe.wait_ge(attn_done, m)
                    for t in range(TC):
                        for h in range(2):
                            o = pair[3][:, t // 3, (t % 3 * 2 + h) * VW:(t % 3 * 2 + h + 1) * VW]
                            for half in range(2):
                                ins = nc.tensor.matmul(o, qp_sb[p % 2][:, 2 * h + half, t * P:(t + 1) * P],
                                                       kv[:, p, 2 * h + half, :], start=(half == 0), stop=(half == 1))
                    ins.then_inc(o_full, 1)

                def turn_a(t):
                    pe.wait_ge(alo_ready, c * TC + t + 1)
                    if t:
                        pe.wait_ge(aT_hi, c * TC + t)
                        pe.wait_ge(aT_lo, c * TC + t)
                    turn(bank16(6), bank16(7), ahi[t % 2], alo[t % 2]).then_inc(atr_full, 1)

                if more:
                    q_up(c + 1, 0)
                turn_a(0)
                for t in range(TC):
                    if t + 1 < TC:
                        turn_a(t + 1)
                    else:
                        pe.wait_ge(aT_hi, c * TC + t + 1)
                        pe.wait_ge(aT_lo, c * TC + t + 1)
                    s, j = q_use[("y", t)]
                    pe.wait_ge(qp_free[s], c * q_uses[s] + j + 1)
                    for k in range(K):
                        ins = mm_split(bank_halves(1 + s, HD), lambda k, a: aT[a][t % 2][:, k * P:(k + 1) * P],
                                       lambda k, b, half: p_w(k, b)[:, half * HD:(half + 1) * HD],
                                       k, k == 0, k == K - 1)
                    ins.then_inc(qp_full[s], 1)

            q_up(0, 0)
            with pe.Fori(0, C - 1) as c:
                chunk3(c)
            chunk3(C - 1, False)
            finish_phase(pe, 2)

            pe.wait_ge(flag_ready, 1)
            large = pe.value_load(flag_i[0:1, 0:1], min_val=0, max_val=1)

            def layer(L, seg, rows):
                pe.sem_inc(L.g_full, 2)
                pe.sem_inc(L.tr, 2)

                def add_rows(u, s):
                    for part in range(2):
                        for half in range(2):
                            ins = nc.tensor.matmul(pair[u][:, half, 0:HD], a_hi[u][:, s, :],
                                                   X[part][:, s, half * HD:(half + 1) * HD],
                                                   start=(s == 0 and part == 0),
                                                   stop=(s == T - 1 and part == 1), skip_group_check=True)
                    return ins

                def add_low(*slots):
                    with pe.If(large):
                        for u in slots:
                            for s in range(T):
                                for half in range(2):
                                    nc.tensor.matmul(pair[u][:, half, 0:HD], a_lo[u][:, s, :],
                                                     X[0][:, s, half * HD:(half + 1) * HD], start=False,
                                                     stop=False, skip_group_check=True)

                def turn_g(n, u):
                    pe.wait_ge(L.glo, n + 1)
                    turn(bank16(4), bank16(5), ghi[u], glo[u]).then_inc(L.tr, 1)

                def gather_two():
                    pe.wait_ge(L.alo, 2)
                    for s in range(T):
                        rows(s)
                        if s == T - 1:
                            add_low(0, 1)
                        for u in range(2):
                            ins = add_rows(u, s)
                            if s == T - 1:
                                ins.then_inc(L.g_full, 1)

                def gather(n, u):
                    pe.wait_ge(L.alo, n + 1)
                    for s in range(T):
                        if s == T // 2:
                            turn_g(n - 1, 1 - u)
                        if s == T - 1:
                            add_low(u)
                        ins = add_rows(u, s)
                    ins.then_inc(L.g_full, 1)

                def gather_third():
                    pe.wait_ge(L.alo, 3)
                    pe.wait_ge(L.glo, 1)
                    for s in range(T):
                        if s == T // 3:
                            turn_g(0, 0)
                        if s == 2 * T // 3:
                            pe.wait_ge(L.gT_hi, 1)
                            pe.wait_ge(L.gT_lo, 1)
                            turn_g(1, 1)
                            transform(0, 0, True)
                        if s == T - 1:
                            add_low(0)
                        ins = add_rows(0, s)
                    ins.then_inc(L.g_full, 1)

                def transform(n, u, first=False):
                    pe.wait_ge(L.gT_hi, n + 1)
                    pe.wait_ge(L.gT_lo, n + 1)
                    if not first:
                        pe.wait_ge(L.z_ev, n)
                    for k in range(K):
                        ins = mm_split(bank_halves(3, HD), lambda k, a: gT[a][u][:, k * P:(k + 1) * P],
                                       lambda k, b, half: gnn_w(k, b)[:, half * HD:(half + 1) * HD],
                                       k, k == 0, k == K - 1)
                    ins.then_inc(L.z_full, 1)

                gather_two()
                weights_ready(pe, seg)
                gather_third()
                transform(1, 1)
                with pe.Fori(0, (T - 3) // 2) as i:
                    gather(2 * i + 3, 1)
                    transform(2 * i + 2, 0)
                    gather(2 * i + 4, 0)
                    transform(2 * i + 3, 1)
                turn_g(T - 1, 0)
                transform(T - 1, 0)

            layer(L1, G1_W, lambda s: pe.wait_ge(pre_lo, s + 1))
            finish_phase(pe, 3)
            layer(L2, G2_W, lambda s: pe.wait_ge(X_in[s // TC], 32) if s % TC == 0 else None)
            finish_phase(pe, 4)

            pe.sem_inc(f_tr, 2)

            def f_turn(n, u):
                pe.wait_ge(f_lo, n + 1)
                turn(bank16(0), bank16(1), fhi[u], flo[u]).then_inc(f_tr, 1)

            def f_up(n, u):
                pe.wait_ge(fT_hi, n + 1)
                pe.wait_ge(fT_lo, n + 1)
                for k in range(K):
                    for m, (a, b) in enumerate(((0, 0), (0, 1), (1, 0))):
                        for dst, lo, hi in ((bank(2), 0, 512), (bank(3), 512, 1024), (bank(4)[:, 384:384 + NX], HB, HB + NX)):
                            ins = nc.tensor.matmul(dst, fT[a][u][:, k * P:(k + 1) * P], w_in(k, b)[:, lo:hi],
                                                   start=(k == 0 and m == 0), stop=(k == K - 1 and m == 2))
                ins.then_inc(f_h, 1)

            def f_mturn(n, u):
                pe.wait_ge(f_mask, n + 1)
                turn(bank16(0), bank16(1), m_hi.rearrange("p e i -> p (e i)"), m_lo.rearrange("p e i -> p (e i)"), NX)\
                    .then_inc(f_mtr, 1)

            def f_down(n, u, first=False):
                pe.wait_ge(mT_hi, n + 1)
                pe.wait_ge(mT_lo, n + 1)
                if not first:
                    pe.wait_ge(f_out, n)
                for e in range(NX):
                    ins = mm_split(bank_halves(3, HD), lambda e, a: mT[a][u][:, e * P:(e + 1) * P],
                                   lambda e, b, half: w_out(e, b)[:, half * HD:(half + 1) * HD],
                                   e, e == 0, e == NX - 1)
                ins.then_inc(f_y, 1)

            f_turn(0, 0)
            weights_ready(pe, FIN_W)
            f_up(0, 0)
            f_turn(1, 1)
            f_mturn(0, 0)
            f_up(1, 1)
            pe.wait_ge(mT_hi, 1)
            pe.wait_ge(mT_lo, 1)
            f_turn(2, 0)
            weights_ready(pe, FOUT_W)
            f_down(0, 0, True)
            f_mturn(1, 1)

            def f_body(n, u):
                f_up(n, u)
                pe.wait_ge(mT_hi, n)
                pe.wait_ge(mT_lo, n)
                f_turn(n + 1, 1 - u)
                f_down(n - 1, 1 - u)
                f_mturn(n, u)

            with pe.Fori(0, (T - 3) // 2) as i:
                f_body(2 * i + 2, 0)
                f_body(2 * i + 3, 1)
            f_up(T - 1, 0)
            f_down(T - 2, 1)
            f_mturn(T - 1, 0)
            f_down(T - 1, 0)


def kernel(**inputs):
    import numpy as _np
    import concourse.bacc as _bacc
    from concourse.bass_utils import run_bass_kernel_spmd as _run

    a = {k: _np.asarray(v) for k, v in inputs.items()}
    x = _np.zeros((NP, D), _np.float32)
    x[:N] = a["x"]
    loops = _np.arange(NP, dtype=_np.int32)
    pad = _np.full(ET * P - E - NP, NP - 1, _np.int32)
    src = _np.concatenate([a["src"].astype(_np.int32), loops, pad])
    dst = _np.concatenate([a["dst"].astype(_np.int32), loops, pad])
    arrays = {
        "x": x,
        "src_row": src.reshape(P, ET), "dst_row": dst.reshape(P, ET),
        "src_col": src.reshape(ET, P).T, "dst_col": dst.reshape(ET, P).T,
        "w_qkv": a["L0_mix_W_qkv"], "w_proj": a["L0_mix_W_proj"],
        "b_proj": a["L0_mix_b_proj"].reshape(1, D), "gamma": a["L0_mix_gamma"].reshape(1, D),
        "beta": a["L0_mix_beta"].reshape(1, D), "rf_t": a["L0_mix_random_features"].T,
        "g1_t": a["L0_gnn_W1"].T, "b1": a["L0_gnn_b1"].reshape(1, D),
        "g2_t": a["L0_gnn_W2"].T, "b2": a["L0_gnn_b2"].reshape(1, D),
        "ffn_in": _np.concatenate([a["L0_ffn_w1"].transpose(1, 0, 2).reshape(D, HB), a["L0_ffn_router_w"].T], axis=1),
        "ffn_out": a["L0_ffn_w2"].reshape(HB, D),
    }
    arrays = {f"in_{k}": _np.ascontiguousarray(v) for k, v in arrays.items()}
    nc = _bacc.Bacc("TRN2", target_bir_lowering=False, num_devices=1)
    args = {k[3:]: nc.dram_tensor(k, v.shape, mybir.dt.from_np(v.dtype), kind="ExternalInput").ap()
            for k, v in arrays.items()}
    out = nc.dram_tensor("out_rows", (NP, D), F32, kind="ExternalOutput").ap()
    build(nc, out=out, **args)
    r = _run(nc, [arrays], core_ids=[0])
    return r.results[0]["out_rows"][:N]
```

```python
from contextlib import ExitStack

import numpy as np

import concourse.bass as bass
from concourse import mybir

F32 = mybir.dt.float32
F16 = mybir.dt.float16
I32 = mybir.dt.int32
ALU = mybir.AluOpType
ACT = mybir.ActivationFunctionType
AXX = mybir.AxisListType.X

P = 128
N = 3125
D = 768
T = -(-N // P)
NP = T * P
K = D // P
HD = D // 2
H, DH, M = 12, 64, 256
PAIRS = H // 2
TC = 5
C = T // TC
CW = TC * P
HW = CW // 2
VW = DH + 2
UNITS = C * PAIRS
E = 50000
EPU = 14
ET = UNITS * EPU
G = 2
EARLIER = 1024.0
NX, NI = 8, 128
HB = NX * NI
CELLS = NP * NP
FAR = float(1 << 24)
LN_EPS = 1e-5
COUNT_EXACT = 2048.0


def over_tiles(eng, body, last=T):
    body(0, 0, 0)
    body(1, 1, 0)
    body(2, 0, 1)
    with eng.Fori(0, (last - 3) // 2) as i:
        body(2 * i + 3, 1, i + 1)
        body(2 * i + 4, 0, i + 2)


def over_rows(eng, body, last=T):
    for q in range(4):
        body(q, q, 0)
    with eng.Fori(1, last // 4) as i:
        for q in range(4):
            body(4 * i + q, q, i)
    body(last - 1, 0, last // 4)


def reused(i):
    return not isinstance(i, int) or i > 0


class Chain:

    def __init__(self, eng, sem, base=0):
        self.eng, self.sem, self.n, self.base = eng, sem, 0, base

    def link(self, ins):
        self.n += 1
        ins.then_inc(self.sem, 1)
        self.eng.wait_ge(self.sem, self.base + self.n)


def build(nc, x, src_row, dst_row, src_col, dst_col, w_qkv, w_proj, b_proj, gamma, beta, rf_t,
          g1_t, b1, g2_t, b2, ffn_in, ffn_out, out):
    ctx = ExitStack()
    with ctx:
        sem = lambda name: ctx.enter_context(nc.semaphore(name))
        dram = lambda name, shape, dt=F32: nc.dram_tensor(name, shape, dt, kind="Internal").ap()

        cells = dram("cells", [CELLS, 1])
        cells_t = cells.rearrange("(t p f) o -> t p (f o)", t=T, p=P)
        key_dram = dram("key_dram", [UNITS, EPU * P])
        xn_dram = dram("xn_dram", [NP, D])
        y_dram = dram("y_dram", [NP, D])
        x2_dram = dram("x2_dram", [NP, D])
        hhi_dram = dram("hhi_dram", [NP, D], F16)
        hlo_dram = dram("hlo_dram", [NP, D], F16)

        arena = ctx.enter_context(nc.sbuf_tensor("arena", [P, 53000], F32))

        def at(off, *shape, dt=F32):
            n = int(np.prod(shape))
            if dt == F16:
                ap = arena[:, off:off + (n + 1) // 2].bitcast(F16)[:, 0:n]
            else:
                ap = arena[:, off:off + n]
                if dt != F32:
                    ap = ap.bitcast(dt)
            if len(shape) == 2:
                ap = ap.rearrange("p (a b) -> p a b", a=shape[0])
            if len(shape) == 3:
                ap = ap.rearrange("p (a b c) -> p a b c", a=shape[0], b=shape[1])
            return ap

        RX, RT, RW, WST, RS = 0, 19200, 38400, 47616, 50688
        s_at = [RS]

        def small(*shape, dt=F32):
            n = int(np.prod(shape))
            n = (n + 1) // 2 if dt == F16 else n
            off = s_at[0]
            s_at[0] += n
            assert s_at[0] <= 53000
            return at(off, *shape, dt=dt)

        rfa, rfb = small(M), small(M)
        ident = small(P, dt=F16)
        iota = small(P, dt=F16)
        earlier = small(G, G * P)
        dst_lo16, dst_hi16 = small(ET, dt=F16), small(ET, dt=F16)
        valid = small(T)
        ones60 = small(TC * H)
        iota8 = small(NX)
        deg = small(26)
        dinv = small(T)
        epsb = small(2)
        mvy = small(T, 2)
        ry = small(T)
        mv2 = small(T, 2)
        r2 = small(T)
        t25 = small(4, T)
        sums = small(EPU)
        skip = small(EPU)
        bst = small(2, 12)
        mvt = small(TC, 2)
        bits = small(2, 16)
        flag_f, flag_i = small(2), small(2, dt=I32)
        stage = [at(WST + 1536 * u, 1536) for u in range(2)]
        stage_g1 = [at(RT + 14336 + D * u, D) for u in range(2)]
        stage_ffn = [at(RX + 12336 + 1536 * u, 1536) for u in range(2)]

        kcol, idx_all, val_all = at(RX, ET), at(RX + 420, ET, dt=I32), at(RX + 840, ET)
        idx_b, val_b = at(RX + 1260, EPU, dt=I32), at(RX + 1274, EPU)
        eint = [at(RX + 1300 + ET * i, ET, dt=I32) for i in range(8)]
        krow = at(RX + 4660, ET)
        ktmp = at(RX + 5080, ET)
        zeros = at(RX + 5500, NP)
        x_in = [at(RX + 13308 + D * q, D) for q in range(4)]
        xn = [at(RX + 10236 + D * u, D) for u in range(2)]
        xhi = [at(RX + 11772 + HD * u, D, dt=F16) for u in range(2)]
        xlo = [at(RX + 12540 + HD * u, D, dt=F16) for u in range(2)]
        xT = [at(RT + 9600 * part, K, NP, dt=F16) for part in range(2)]
        kk = [at(RX + 1300 + 2 * CW * u, 2, CW) for u in range(2)]
        kp_sb = [at(RX + 3860 + 512 * u, 512) for u in range(2)]
        junk = [at(RX + 4900 + G * P * u, G * P) for u in range(2)]
        kb = [at(RX + 8700 + EPU * P * u, EPU * P) for u in range(2)]
        oh_lo = at(RX + 12284, EPU, P, dt=F16)
        oh_hi = at(RX + 13180, EPU, 26, dt=F16)
        vals = at(RX + 13400, TC, H, VW)
        kv = at(RX + 17430, PAIRS, 4, VW)
        qp_sb = [at(RX + 3860 + 4 * CW * u, 4, CW) for u in range(2)]
        attn = at(RX + 8980, TC, D)
        ahi = [at(RX + 12820 + HD * u, D, dt=F16) for u in range(2)]
        alo = [at(RX + 13588 + HD * u, D, dt=F16) for u in range(2)]
        aT = [[at(RX + 14356 + HD * (2 * part + u), D, dt=F16) for u in range(2)] for part in range(2)]
        xl3 = [at(RX + 15892 + D * u, D) for u in range(2)]
        y_sb = [at(WST + D * u, D) for u in range(2)]
        brow3 = at(WST + 1536, D)
        rden = at(WST + 2304, TC, 2)
        X = [at(RX + 9600 * part, T, D, dt=F16) for part in range(2)]
        a_in = [at(RT + NP * u, NP) for u in range(2)]
        a_hi = [at(RT + 6400 + 1600 * u, T, P, dt=F16) for u in range(2)]
        a_lo = [at(RT + 9600 + 1600 * u, T, P, dt=F16) for u in range(2)]
        ghi = [at(RT + 12800 + HD * u, D, dt=F16) for u in range(2)]
        glo = [at(RT + 13568 + HD * u, D, dt=F16) for u in range(2)]
        gT = [[at(RT + 14336 + HD * (2 * part + u), D, dt=F16) for u in range(2)] for part in range(2)]
        zt = [at(RT + 15872 + D * u, D) for u in range(2)]
        zr = [at(RT + 17408 + D * u, D) for u in range(2)]
        gnn_w = lambda k, part: at(RW + 768 * k + HD * part, D, dt=F16)
        zhi = [at(RW + 4608 + HD * u, D, dt=F16) for u in range(2)]
        zlo = [at(RW + 5376 + HD * u, D, dt=F16) for u in range(2)]
        xl = [at(RW + 6144 + D * u, D) for u in range(2)]
        yl = [at(RW + 7680 + D * u, D) for u in range(2)]
        xl4 = [at(RT + 15872 + D * q, D) for q in range(4)]
        row_a, row_g = at(WST, D), at(WST + D, D)
        row_t = at(WST + 2 * D, D)
        w_in = lambda k, part: at(RX + 1032 * k + 516 * part, HB + NX, dt=F16)
        w_out = lambda e, part: at(RX + 6192 + 768 * e + HD * part, D, dt=F16)
        fx = [at(RT + D * u, D) for u in range(2)]
        fr = [at(RT + D * (2 + u), D) for u in range(2)]
        fn = [at(RT + 3072 + D * u, D) for u in range(2)]
        fhi = [at(RT + 4608 + HD * u, D, dt=F16) for u in range(2)]
        flo = [at(RT + 5376 + HD * u, D, dt=F16) for u in range(2)]
        fT = [[at(RT + 6144 + HD * (2 * part + u), D, dt=F16) for u in range(2)] for part in range(2)]
        hsel_all = at(RT + 7680, NX, NI)
        hsel, hact = at(RT + 8704, NI), at(RT + 8832, NI)
        act_hi, act_lo = at(RT + 8960, NI, dt=F16), at(RT + 9024, NI, dt=F16)
        m_hi, m_lo = at(RT + 9088, NX, NI, dt=F16), at(RT + 9600, NX, NI, dt=F16)
        mT = [[at(RT + 10112 + 512 * (2 * part + u), HB, dt=F16) for u in range(2)] for part in range(2)]
        fo = [at(RX + 15408 + D * u, D) for u in range(2)]
        lg, top, mask = at(RX + 16950, NX), at(RX + 16958, NX), at(RX + 16966, NX)
        topi = at(RX + 16974, NX, dt=mybir.dt.uint32)
        topf, esel, mask16 = at(RX + 16982, NX), at(RX + 16990, 2), at(RX + 16994, NX, dt=F16)
        nmax = at(RX + 17000, 2)

        pair = [ctx.enter_context(nc.psum_tensor(f"pair{i}", [P, 2, 512], F32)) for i in range(4)]
        bank = lambda b: pair[b // 2][:, b % 2, :]
        bank16 = lambda b: pair[b // 2][:, b % 2, :].bitcast(F16)
        wide = lambda i: pair[i][:, :, 0:HD]
        halves = lambda ap: ap.rearrange("p (a b) -> p a b", a=2)

        KV_W, Q_W, P_W, G1_W, G2_W, FIN_W, FOUT_W = range(7)
        items = []
        for k in range(K):
            off = RW + 1536 * k
            items.append((KV_W, w_qkv[k * P:(k + 1) * P, D:3 * D], 2 * D,
                          at(off, 2 * D, dt=F16), at(off + D, 2 * D, dt=F16)))
        for j, w in enumerate((w_qkv[:, 0:D], w_proj)):
            for k in range(K):
                off = RW + 4608 * j + 768 * k
                items.append(((Q_W, P_W)[j], w[k * P:(k + 1) * P, :], D, at(off, D, dt=F16), at(off + HD, D, dt=F16)))
        for seg, w in ((G1_W, g1_t), (G2_W, g2_t)):
            for k in range(K):
                items.append((seg, w[k * P:(k + 1) * P, :], D, gnn_w(k, 0), gnn_w(k, 1)))
        for k in range(K):
            items.append((FIN_W, ffn_in[k * P:(k + 1) * P, :], HB + NX, w_in(k, 0), w_in(k, 1)))
        for e in range(NX):
            items.append((FOUT_W, ffn_out[e * P:(e + 1) * P, :], D, w_out(e, 0), w_out(e, 1)))
        kv_w = lambda k, part: items[k][3 + part]
        q_w = lambda k, part: items[K + k][3 + part]
        p_w = lambda k, part: items[2 * K + k][3 + part]

        w_in_sem = [sem("w_in0"), sem("w_in1")]
        w_hi_done, w_lo_done = sem("w_hi_done"), sem("w_lo_done")

        def staged(m):
            rows = {G1_W: stage_g1, FIN_W: stage_ffn, FOUT_W: stage_ffn}.get(items[m][0], stage)
            return rows[m % 2][:, 0:items[m][2]]

        def of(seg):
            return [m for m, item in enumerate(items) if item[0] == seg]

        def load_weights(sp, seg, part=slice(None)):
            for m in of(seg)[part]:
                if m >= 2:
                    sp.wait_ge(w_lo_done, m - 1)
                sp.dma_start(staged(m), items[m][1]).then_inc(w_in_sem[m % 2], 16)

        def split_hi(act, seg, part=slice(None)):
            for m in of(seg)[part]:
                act.wait_ge(w_in_sem[m % 2], 16 * (m // 2 + 1))
                nc.scalar.copy(items[m][3], staged(m)).then_inc(w_hi_done, 1)

        def split_lo(dve, seg, part=slice(None)):
            for m in of(seg)[part]:
                dve.wait_ge(w_hi_done, m + 1)
                nc.vector.tensor_tensor(items[m][4], staged(m), items[m][3], ALU.subtract).then_inc(w_lo_done, 1)

        def weights_ready(eng, seg):
            eng.wait_ge(w_lo_done, of(seg)[-1] + 1)

        phase_done = sem("phase_done")
        consts, consts_in, zeros_ready = sem("consts"), sem("consts_in"), sem("zeros_ready")
        edges_in, key_made, key_stored = sem("edges_in"), sem("key_made"), sem("key_stored")
        cleared, scattered = [sem("cleared0"), sem("cleared1")], sem("scattered")
        x_ld = [sem(f"x_ld{q}") for q in range(4)]
        xn_st = [sem("xn_st0"), sem("xn_st1")]
        var_ready, sd_ready, xn_ready = sem("var_ready"), sem("sd_ready"), sem("xn_ready")
        hi_ready, lo_ready, tr_done = sem("hi_ready"), sem("lo_ready"), sem("tr_done")
        ev_hi, ev_lo = sem("ev_hi"), sem("ev_lo")
        dve_done, mvy_done = sem("dve_done"), sem("mvy_done")
        dve_links = [0]

        def links(each, times=1):
            dve_links[0] += each * times
            return dve_links[0] - each * times

        slot_full = [sem("slot_full0"), sem("slot_full1")]
        slot_free = [sem("slot_free0"), sem("slot_free1")]
        vone_ready, kk_sq, kk_cp = sem("vone_ready"), sem("kk_sq"), sem("kk_cp")
        kp_full, kp_exp, kv_full, kv_free = sem("kp_full"), sem("kp_exp"), sem("kv_full"), sem("kv_free")
        kb_in, scan_done = [sem("kb_in0"), sem("kb_in1")], sem("scan_done")
        unit_scanned, pool_copied, idx_ready = sem("unit_scanned"), sem("pool_copied"), sem("idx_ready")
        oh_ready, deg_full, deg_free = sem("oh_ready"), sem("deg_full"), sem("deg_free")

        spacer = {}

        def finish_phase(eng, k):
            eng.drain().then_inc(phase_done, 1)
            eng.wait_ge(phase_done, 4 * (k + 1))

        def apart(eng):
            eng.sem_inc(spacer[eng], 1)

        def mm_split(dst, left, right, k, start, stop):
            for n, (a, b) in enumerate(((0, 0), (0, 1), (1, 0))):
                for half in range(2):
                    ins = nc.tensor.matmul(dst[half], left(k, a), right(k, b, half),
                                           start=start and n == 0, stop=stop and n == 2)
            return ins

        def bank_halves(i, width):
            return [pair[i][:, h, 0:width] for h in range(2)]

        def all_cleared(eng):
            for u in range(2):
                eng.wait_ge(cleared[u], 16 * ((T + 1 - u) // 2))

        slot_use, uses = {}, [0, 0]
        for n, key in enumerate([("v", t) for t in range(TC)] + [("k", p) for p in range(PAIRS)]):
            slot_use[key] = (n % 2, uses[n % 2])
            uses[n % 2] += 1

        q_use, q_uses = {}, [0, 0]
        for n, key in enumerate([("q", p, g) for p in range(PAIRS) for g in range(4)] + [("y", t) for t in range(TC)]):
            q_use[key] = (n % 2, q_uses[n % 2])
            q_uses[n % 2] += 1
        y_use, y_uses = {}, [0, 0]
        for t in range(TC):
            y_use[t] = (t % 2, y_uses[t % 2])
            y_uses[t % 2] += 1
        qt_full, qt_free, qq_sq, qq_cp = sem("qt_full"), sem("qt_free"), sem("qq_sq"), sem("qq_cp")
        qp_full, qp_free = [sem("qp_full0"), sem("qp_full1")], [sem("qp_free0"), sem("qp_free1")]
        qp_exp, o_full, attn_done = sem("qp_exp"), sem("o_full"), sem("attn_done")
        kv_scaled, vals_clear = sem("kv_scaled"), sem("vals_clear")
        ahi_ready, alo_ready, atr_full = sem("ahi_ready"), sem("alo_ready"), sem("atr_full")
        aT_hi, aT_lo = sem("aT_hi"), sem("aT_lo")
        xl_in, xl_used = [sem("xl_in0"), sem("xl_in1")], [sem("xl_used0"), sem("xl_used1")]
        y_ready, y_st = sem("y_ready"), [sem("y_st0"), sem("y_st1")]
        rows_in = sem("rows_in")
        pre_ld = [sem(f"pre_ld{q}") for q in range(4)]
        pre_hi, pre_lo = sem("pre_hi"), sem("pre_lo")
        sq_asked, sq_done, flag_max, flag_ready = sem("sq_asked"), sem("sq_done"), sem("flag_max"), sem("flag_ready")
        X_in = [sem(f"X_in{c}") for c in range(C)]

        class Layer:
            def __init__(self, name):
                s = lambda what: sem(f"{name}_{what}")
                self.a_ld = [s("a_ld0"), s("a_ld1")]
                self.ahi, self.alo, self.g_full = s("ahi"), s("alo"), s("g_full")
                self.ghi, self.glo, self.tr = s("ghi"), s("glo"), s("tr")
                self.gT_hi, self.gT_lo, self.z_full, self.z_ev = s("gT_hi"), s("gT_lo"), s("z_full"), s("z_ev")
                self.relu, self.zhi, self.zlo = s("relu"), s("zhi"), s("zlo")
                self.st = [s("st0"), s("st1")]
                if name == "l2":
                    self.x_ld = [s("x_ld0"), s("x_ld1")]
                    self.done = s("done")

        L1, L2 = Layer("l1"), Layer("l2")
        f_ld, fr_ld = [sem("f_ld0"), sem("f_ld1")], [sem("fr_ld0"), sem("fr_ld1")]
        f_norm, f_hi, f_lo, f_tr, fT_hi, fT_lo = [sem(f"f_{n}") for n in ("norm", "hi", "lo", "tr", "T_hi", "T_lo")]
        f_h, f_hsel, f_act, f_ahi, f_mask, f_mtr = [sem(f"f_{n}") for n in ("h", "hsel", "act", "ahi", "mask", "mtr")]
        mT_hi, mT_lo, f_y, f_out = sem("mT_hi"), sem("mT_lo"), sem("f_y"), sem("f_out")
        f_st = [sem("f_st0"), sem("f_st1")]

        block = ctx.enter_context(nc.Block())

        @block.sync
        def _(sp):
            spacer[sp] = sem("sp_spacer")
            for i, a in enumerate((src_row, dst_row, src_col, dst_col)):
                sp.dma_start(eint[2 * i], a).then_inc(edges_in, 16)
            sp.dma_start(rfa[0:DH, :], rf_t).then_inc(consts_in, 16)
            sp.dma_start(rfb[DH:P, :], rf_t).then_inc(consts_in, 16)
            for q in range(4):
                sp.dma_start(x_in[q], x[q * P:(q + 1) * P, :]).then_inc(x_ld[q], 16)
            load_weights(sp, KV_W)
            sp.wait_ge(key_made, 1)
            sp.dma_start(key_dram.rearrange("u e -> (u e)").rearrange("(p f) -> p f", p=P), krow).then_inc(key_stored, 16)

            def load_x(n, q, i):
                sp.wait_ge(xn_ready, n + 1)
                sp.dma_start(x_in[q], x[bass.ds(P * (n + 4), P), :]).then_inc(x_ld[q], 16)

            over_rows(sp, load_x, T - 4)
            sp.wait_ge(key_stored, 16)
            finish_phase(sp, 0)

            for u in range(2):
                sp.dma_start(kb[u], key_dram[u:u + 1, :].partition_broadcast(P)).then_inc(kb_in[u], 16)
            with sp.Fori(0, UNITS // 2 - 1) as i:
                for u in range(2):
                    sp.wait_ge(unit_scanned, 2 * i + u + 1)
                    sp.dma_start(kb[u], key_dram[bass.ds(2 * i + u + 2, 1), :].partition_broadcast(P))\
                        .then_inc(kb_in[u], 16)
            load_weights(sp, Q_W, slice(0, 2))
            finish_phase(sp, 1)

            load_weights(sp, Q_W, slice(2, None))
            load_weights(sp, P_W)
            weights_ready(sp, P_W)
            sp.dma_start(brow3, b_proj.partition_broadcast(P)).then_inc(rows_in, 16)

            def chunk3(c, more=True):
                for t in range(TC + 1):
                    if not more and t == 2:
                        sp.wait_ge(qt_full, C * PAIRS)
                        sp.wait_ge(scattered, 16 * ET)
                        for u in range(2):
                            sp.dma_start(a_in[u], cells_t[u]).then_inc(L1.a_ld[u], 16)
                        load_weights(sp, G1_W, slice(0, 2))
                    if t < TC:
                        s, j = y_use[t]
                        sp.wait_ge(xl_used[s], c * y_uses[s] + j + 1)
                        sp.dma_start(xl3[s], xn_dram[bass.ds(c * CW + t * P, P), :]).then_inc(xl_in[s], 16)
                    if t:
                        sp.wait_ge(y_ready, c * TC + t)
                        sp.dma_start(y_dram[bass.ds(c * CW + (t - 1) * P, P), :], y_sb[y_use[t - 1][0]])\
                            .then_inc(y_st[y_use[t - 1][0]], 16)
                    if not more and t >= TC - 1:
                        load_weights(sp, G1_W, slice(2 * (t - TC) + 4, 2 * (t - TC) + 6))

            with sp.Fori(0, C - 1) as c:
                chunk3(c)
            chunk3(C - 1, False)
            sp.wait_ge(y_st[0], 16 * C * y_uses[0])
            sp.wait_ge(y_st[1], 16 * C * y_uses[1])
            for u in range(4):
                sp.dma_start(xl4[u], xn_dram[u * P:(u + 1) * P, :]).then_inc(pre_ld[u], 16)

            finish_phase(sp, 2)

            def load_pre(n, q, i):
                sp.wait_ge(pre_lo, n + 1)
                sp.dma_start(xl4[q], xn_dram[bass.ds(P * (n + 4), P), :]).then_inc(pre_ld[q], 16)

            over_rows(sp, load_pre, T - 4)
            sp.dma_start(row_a, b1.partition_broadcast(P)).then_inc(rows_in, 16)

            def load_counts(L):
                for u in range(2):
                    sp.dma_start(a_in[u], cells_t[u]).then_inc(L.a_ld[u], 16)

            def next_counts(L, n, u):
                sp.wait_ge(L.alo, n + 1)
                sp.dma_start(a_in[u], cells_t[bass.ds(n + 2, 1)].rearrange("t p f -> (t p) f"))\
                    .then_inc(L.a_ld[u], 16)

            over_tiles(sp, lambda n, u, i: next_counts(L1, n, u), T - 2)

            sp.wait_ge(L1.alo, T)
            load_counts(L2)
            sp.wait_ge(L1.g_full, T + 2)
            for c in range(C):
                for u in range(2):
                    sp.wait_ge(L1.st[u], 32 * ((TC * (c + 1) + 1 - u) // 2))
                for i, src in enumerate((hhi_dram, hlo_dram)):
                    sp.dma_start(X[i][:, c * TC:(c + 1) * TC, :],
                                 src[c * CW:(c + 1) * CW, :].rearrange("(t p) d -> p t d", p=P)).then_inc(X_in[c], 16)
            finish_phase(sp, 3)
            for u in range(2):
                sp.dma_start(xl[u], x[u * P:(u + 1) * P, :]).then_inc(L2.x_ld[u], 16)
                sp.dma_start(yl[u], y_dram[u * P:(u + 1) * P, :]).then_inc(L2.x_ld[u], 16)
            load_weights(sp, G2_W)
            weights_ready(sp, G2_W)
            for dst, src in ((row_a, b2), (row_g, gamma), (row_t, beta)):
                sp.dma_start(dst, src.partition_broadcast(P)).then_inc(rows_in, 16)

            def load_l2(n, u, i):
                next_counts(L2, n, u)
                sp.wait_ge(L2.z_ev, n + 1)
                sp.dma_start(xl[u], x[bass.ds(P * (n + 2), P), :]).then_inc(L2.x_ld[u], 16)
                sp.dma_start(yl[u], y_dram[bass.ds(P * (n + 2), P), :]).then_inc(L2.x_ld[u], 16)

            over_tiles(sp, load_l2, T - 2)

            sp.wait_ge(L2.g_full, T + 2)
            for u in range(2):
                sp.wait_ge(L2.st[u], 16)
                sp.dma_start(fx[u], x2_dram[u * P:(u + 1) * P, :]).then_inc(f_ld[u], 16)
                sp.dma_start(fr[u], x2_dram[u * P:(u + 1) * P, :]).then_inc(fr_ld[u], 16)
            load_weights(sp, FIN_W, slice(0, 4))
            finish_phase(sp, 4)
            load_weights(sp, FIN_W, slice(4, K))
            load_weights(sp, FOUT_W)

            def load_f(n, u, i):
                sp.wait_ge(f_norm, n + 1)
                sp.dma_start(fx[u], x2_dram[bass.ds(P * (n + 2), P), :]).then_inc(f_ld[u], 16)
                sp.wait_ge(f_out, n + 1)
                sp.dma_start(fr[u], x2_dram[bass.ds(P * (n + 2), P), :]).then_inc(fr_ld[u], 16)

            over_tiles(sp, load_f, T - 2)

        @block.gpsimd
        def _(pool):
            spacer[pool] = sem("pool_spacer")
            made = Chain(pool, sem("pool_chain"))
            nc.gpsimd.memset(zeros, 0.0).then_inc(zeros_ready, 1)
            made.link(nc.gpsimd.memset(ident, 0.0))
            made.link(nc.gpsimd.affine_select(out=ident, in_=ident, compare_op=ALU.not_equal, fill=1.0, base=0,
                                              pattern=[[-1, P]], channel_multiplier=1))
            made.link(nc.gpsimd.iota(iota, pattern=[[1, P]], base=0, channel_multiplier=0,
                                     allow_small_or_imprecise_dtypes=True))
            made.link(nc.gpsimd.iota(iota8, pattern=[[1, NX]], base=0, channel_multiplier=0,
                                     allow_small_or_imprecise_dtypes=True))
            made.link(nc.gpsimd.memset(valid, 1.0))
            made.link(nc.gpsimd.affine_select(out=valid, in_=valid, compare_op=ALU.is_ge, fill=0.0, base=N - 1,
                                              pattern=[[-P, T]], channel_multiplier=-1))
            made.link(nc.gpsimd.memset(earlier, 1.0))
            for q in range(G):
                made.link(nc.gpsimd.affine_select(out=earlier[:, q, :], in_=earlier[:, q, :], compare_op=ALU.is_ge,
                                                  fill=1.0 + EARLIER, base=-q * P, pattern=[[1, G * P]],
                                                  channel_multiplier=-1))
            made.link(nc.gpsimd.memset(rfa[DH:P, :], -0.5))
            made.link(nc.gpsimd.memset(rfb[0:DH, :], -0.5))
            made.link(nc.gpsimd.memset(ones60, 1.0))
            made.link(nc.gpsimd.memset(epsb, LN_EPS))
            made.link(nc.gpsimd.memset(deg, 0.0))
            pool.wait_ge(consts_in, 32)
            nc.gpsimd.memset(bits, 0.0).then_inc(consts, 1)

            def scatter(b):
                pool.wait_ge(idx_ready, b + 1)
                apart(pool)
                if reused(b):
                    pool.wait_ge(scattered, b * (16 * EPU))
                    apart(pool)
                nc.gpsimd.tensor_copy(idx_b, idx_all[:, bass.ds(b * EPU, EPU)]).then_inc(pool_copied, 1)
                nc.gpsimd.tensor_copy(val_b, val_all[:, bass.ds(b * EPU, EPU)]).then_inc(pool_copied, 1)
                pool.wait_ge(pool_copied, 2 * b + 2)
                apart(pool)
                for j in range(EPU):
                    if j % G == 0 and j:
                        pool.wait_ge(scattered, b * (16 * EPU) + 16 * j)
                        apart(pool)
                    nc.gpsimd.indirect_dma_start(
                        cells, bass.IndirectOffsetOnAxis(ap=idx_b[:, j:j + 1], axis=0), val_b[:, j:j + 1], None,
                        bounds_check=CELLS - 1, oob_is_err=False, compute_op=ALU.add).then_inc(scattered, 16)

            pool.wait_ge(zeros_ready, 1)
            pool.wait_ge(lo_ready, T)
            for n in range(T):
                if n >= 2:
                    pool.wait_ge(cleared[n % 2], 16 * (n // 2))
                pool.dma_start(cells_t[n], zeros).then_inc(cleared[n % 2], 16)
            all_cleared(pool)
            scatter(0)
            with pool.Fori(1, UNITS) as b:
                scatter(b)
            pool.wait_ge(scattered, 16 * ET)
            pool.wait_ge(flag_max, 1)
            nc.gpsimd.partition_all_reduce(flag_f[:, 1:2], flag_f[:, 0:1], P, bass.bass_isa.ReduceOp.max)\
                .then_inc(flag_max, 1)

        @block.scalar
        def _(act):
            spacer[act] = sem("act_spacer")
            act.wait_ge(zeros_ready, 1)
            act.wait_ge(consts, 1)
            act.sem_inc(ev_hi, 2)
            split_hi(act, KV_W, slice(0, 2))

            def evict_hi(n):
                act.wait_ge(tr_done, n + 3)
                apart(act)
                nc.scalar.copy(xT[0][:, :, bass.ds(n * P, P)], halves6(bank16u_hi(n))).then_inc(ev_hi, 1)

            halves6 = lambda ap: ap[:, 0:D].rearrange("p (k n) -> p k n", k=K)
            slot_of = {}

            def bank16u_hi(n):
                return bank16(2 * slot_of["prev"])

            def root(n, u):
                act.wait_ge(var_ready, n + 1)
                nc.scalar.activation(bits[:, u, 0:1], bits[:, u, 1:2], ACT.Sqrt).then_inc(sd_ready, 1)

            def ln1(n, u, i):
                if not isinstance(n, int) or n < T - 1:
                    root(n + 1, 1 - u)
                if reused(n):
                    slot_of["prev"] = 1 - u
                    evict_hi(n - 1)
                act.wait_ge(xn_ready, n + 1)
                act.wait_ge(tr_done, n + 1)
                nc.scalar.copy(xhi[u], xn[u]).then_inc(hi_ready, 1)
                act.dma_start(xn_dram[bass.ds(n * P, P), :], xn[u]).then_inc(xn_st[u], 16)
                if isinstance(n, int) and n < 4:
                    split_hi(act, KV_W, slice(n + 2, n + 3))

            root(0, 0)
            over_rows(act, lambda n, q, i: ln1(n, q % 2, i))
            slot_of["prev"] = 0
            evict_hi(T - 1)
            act.wait_ge(xn_st[0], 16 * 13)
            act.wait_ge(xn_st[1], 16 * 12)
            finish_phase(act, 0)

            act.sem_inc(kp_exp, 2)
            act.sem_inc(slot_free[0], 2)
            act.sem_inc(slot_free[1], 2)

            def square_k(c, p):
                act.wait_ge(kk_cp, 2 * (c * PAIRS + p) + 2)
                nc.scalar.activation(kk[p % 2][DH:P, 0, :], kk[p % 2][0:DH, 0, :], ACT.Square).then_inc(kk_sq, 1)
                nc.scalar.activation(kk[p % 2][0:DH, 1, :], kk[p % 2][DH:P, 1, :], ACT.Square).then_inc(kk_sq, 1)

            bank_pair = lambda s: pair[s][:, :, 0:HW]

            act.wait_ge(vals_clear, 1)
            with act.Fori(0, C) as c:
                for t in range(TC):
                    s, j = slot_use[("v", t)]
                    act.wait_ge(slot_full[s], c * uses[s] + j + 1)
                    apart(act)
                    nc.scalar.activation(
                        vals[:, t, :, 0:DH].rearrange("p (a h) d -> p a h d", a=2),
                        wide(s).rearrange("p a (h d) -> p a h d", h=H // 2), ACT.Copy,
                        scale=valid[:, bass.ds(c * TC + t, 1)]).then_inc(slot_free[s], 2)
                square_k(c, 0)
                for p in range(PAIRS):
                    for t in range(TC):
                        q = (p * TC + t) % 2
                        act.wait_ge(kp_full, (c * PAIRS + p) * TC + t + 1)
                        nc.scalar.activation(kp_sb[q], bank(4 + q), ACT.Exp).then_inc(kp_exp, 1)
                        if t == 2 and p + 1 < PAIRS:
                            square_k(c, p + 1)
            all_cleared(act)
            finish_phase(act, 1)

            nc.scalar.activation(t25[:, 0, :], deg[:, 0:T], ACT.Sqrt).then_inc(sq_done, 1)
            split_hi(act, Q_W)
            act.sem_inc(qt_free, 1)
            for s in range(2):
                act.sem_inc(qp_free[s], 1)
                act.sem_inc(xl_used[s], 1)

            def square_q(c, p):
                act.wait_ge(qq_cp, 2 * (c * PAIRS + p) + 2)
                nc.scalar.activation(kk[p % 2][DH:P, 0, :], kk[p % 2][0:DH, 0, :], ACT.Square).then_inc(qq_sq, 1)
                nc.scalar.activation(kk[p % 2][0:DH, 1, :], kk[p % 2][DH:P, 1, :], ACT.Square).then_inc(qq_sq, 1)

            def chunk3(c, first=False, more=True):
                for p in range(PAIRS):
                    for g in range(4):
                        s, j = q_use[("q", p, g)]
                        act.wait_ge(qp_full[s], c * q_uses[s] + j + 1)
                        nc.scalar.activation(qp_sb[p % 2][:, g, :].rearrange("p (a b) -> p a b", a=2),
                                             bank_pair(1 + s), ACT.Exp).then_inc(qp_free[s], 1)
                    act.wait_ge(qp_free[0], c * q_uses[0] + 2 * p + 3)
                    act.wait_ge(qp_free[1], c * q_uses[1] + 2 * p + 3)
                    act.sem_inc(qp_exp, 1)
                    if p + 1 < PAIRS:
                        square_q(c, p + 1)
                    if first:
                        split_hi(act, P_W, slice(p, p + 1))

                def high(t):
                    act.wait_ge(attn_done, (c + 1) * PAIRS)
                    act.wait_ge(atr_full, c * TC + t + 1)
                    nc.scalar.copy(ahi[t % 2], attn[:, t, :]).then_inc(ahi_ready, 1)

                high(0)
                high(1)
                for t in range(TC):
                    act.wait_ge(atr_full, c * TC + t + 3)
                    nc.scalar.copy(aT[0][t % 2], bank16(6)[:, 0:D]).then_inc(aT_hi, 1)
                    if t + 2 < TC:
                        high(t + 2)
                    if t == 1 and more:
                        square_q(c + 1, 0)
                    if not more:
                        if t in (1, 3):
                            counts(L1, t // 2, t // 2, 0)
                        if t in (2, 4):
                            split_hi(act, G1_W, slice(t - 2, t))

            def counts(L, n, u, i):
                act.wait_ge(L.a_ld[u], 16 * i + 16)
                act.wait_ge(L.g_full, n + 1)
                nc.scalar.copy(a_hi[u].rearrange("p a b -> p (a b)"), a_in[u]).then_inc(L.ahi, 1)

            square_q(0, 0)
            chunk3(0, first=True)
            with act.Fori(1, C - 1) as c:
                chunk3(c)
            chunk3(C - 1, more=False)
            split_hi(act, G1_W, slice(4, K))
            finish_phase(act, 2)


            def pre(n, q, i):
                act.wait_ge(pre_ld[q], 16 * i + 16)
                apart(act)
                nc.scalar.activation(X[0][:, bass.ds(n, 1), :].rearrange("p a b -> p (a b)"), xl4[q], ACT.Copy,
                                     scale=dinv[:, bass.ds(n, 1)]).then_inc(pre_hi, 1)

            def layer(L, first, seg):
                def split_g(n, u):
                    act.wait_ge(L.g_full, n + 3)
                    act.wait_ge(L.tr, n + 1)
                    nc.scalar.copy(halves(ghi[u]), wide(u)).then_inc(L.ghi, 1)

                def evict(n, u):
                    act.wait_ge(L.tr, n + 3)
                    nc.scalar.copy(gT[0][u], bank16(4)[:, 0:D]).then_inc(L.gT_hi, 1)

                def finish1(n, u, i):
                    act.wait_ge(L.z_ev, n + 1)
                    apart(act)
                    nc.scalar.activation(zr[u], zt[u], ACT.Relu, scale=dinv[:, bass.ds(n, 1)]).then_inc(L.relu, 1)
                    act.wait_ge(L.relu, n + 3)
                    if reused(i):
                        act.wait_ge(L.st[u], 32 * i)
                    nc.scalar.copy(zhi[u], zr[u]).then_inc(L.zhi, 1)
                    act.wait_ge(L.zhi, n + 1)
                    act.dma_start(hhi_dram[bass.ds(n * P, P), :], zhi[u]).then_inc(L.st[u], 16)
                    act.wait_ge(L.zlo, n + 1)
                    act.dma_start(hlo_dram[bass.ds(n * P, P), :], zlo[u]).then_inc(L.st[u], 16)

                def finish2(n, u, i):
                    act.wait_ge(L.z_ev, n + 1)
                    act.dma_start(x2_dram[bass.ds(n * P, P), :], zt[u]).then_inc(L.st[u], 16)

                def body(n, u, i, more=True):
                    if more:
                        counts(L, n + 1, 1 - u, i if u == 0 else i + 1)
                    if reused(n):
                        evict(n - 1, 1 - u)
                    split_g(n, u)
                    if reused(n):
                        (finish1 if first else finish2)(n - 1, 1 - u, i if u == 1 else i - 1)

                act.sem_inc(L.relu, 2)
                if first:
                    over_rows(act, pre)
                    act.wait_ge(sq_asked, 1)
                    nc.scalar.activation(t25[:, 1, :], mvy[:, :, 1], ACT.Sqrt).then_inc(sq_done, 1)
                else:
                    counts(L, 0, 0, 0)
                    counts(L, 1, 1, 0)
                    split_hi(act, seg)
                body(0, 0, 0, False)
                body(1, 1, 0)
                body(2, 0, 1)
                with act.Fori(0, (T - 5) // 2) as i:
                    body(2 * i + 3, 1, i + 1)
                    body(2 * i + 4, 0, i + 2)
                body(T - 2, 1, T // 2 - 1)
                body(T - 1, 0, T // 2, False)
                evict(T - 1, 0)
                if not first:
                    split_hi(act, FIN_W, slice(0, 2))
                (finish1 if first else finish2)(T - 1, 0, (T - 1) // 2)
                act.wait_ge(L.st[0], (32 if first else 16) * 13)
                act.wait_ge(L.st[1], (32 if first else 16) * 12)

            layer(L1, True, G1_W)
            finish_phase(act, 3)
            layer(L2, False, G2_W)
            act.wait_ge(L2.done, 1)
            nc.scalar.activation(t25[:, 0, :], mv2[:, :, 1], ACT.Sqrt).then_inc(sq_done, 1)
            act.wait_ge(sq_done, 3)
            finish_phase(act, 4)

            def f_high(n, u):
                act.wait_ge(f_norm, n + 1)
                act.wait_ge(f_tr, n + 1)
                nc.scalar.copy(fhi[u], fn[u]).then_inc(f_hi, 1)

            def f_evict(n, u):
                act.wait_ge(f_tr, n + 3)
                nc.scalar.copy(fT[0][u], bank16(0)[:, 0:D]).then_inc(fT_hi, 1)

            def silu(n):
                act.wait_ge(f_hsel, n + 1)
                nc.scalar.activation(hact, hsel, ACT.Silu).then_inc(f_act, 1)
                act.wait_ge(f_act, n + 1)
                nc.scalar.copy(act_hi, hact).then_inc(f_ahi, 1)

            def m_evict(n, u):
                act.wait_ge(f_mtr, n + 1)
                nc.scalar.copy(mT[0][u], bank16(0)).then_inc(mT_hi, 1)

            def store(n, u):
                act.wait_ge(f_out, n + 1)
                act.dma_start(out[bass.ds(n * P, P), :], fo[u]).then_inc(f_st[u], 16)

            f_high(0, 0)
            split_hi(act, FIN_W, slice(2, K))
            f_evict(0, 0)
            split_hi(act, FOUT_W)

            def experts(n, u, i):
                f_high(n + 1, 1 - u)
                f_evict(n + 1, 1 - u)
                silu(n)
                m_evict(n, u)
                if reused(n):
                    store(n - 1, 1 - u)

            over_tiles(act, experts, T - 2)
            for n in (T - 2, T - 1):
                u = n % 2
                if n + 1 < T:
                    f_high(n + 1, 1 - u)
                    f_evict(n + 1, 1 - u)
                silu(n)
                m_evict(n, u)
                store(n - 1, 1 - u)
            store(T - 1, 0)
            act.wait_ge(f_st[0], 16 * 13)
            act.wait_ge(f_st[1], 16 * 12)

        @block.vector
        def _(dve):
            spacer[dve] = sem("dve_spacer")
            e = Chain(dve, dve_done, links(16))
            dve.wait_ge(edges_in, 64)
            for r, (row, key) in enumerate(((0, krow), (4, kcol))):
                s_lo, s_hi, d_lo, d_hi = eint[row + 1], eint[row], eint[row + 3], eint[row + 2]
                for lo, hi in ((s_lo, s_hi), (d_lo, d_hi)):
                    e.link(nc.vector.tensor_scalar(lo, hi, P - 1, None, ALU.bitwise_and))
                    e.link(nc.vector.tensor_scalar(hi, hi, 7, None, ALU.logical_shift_right))
                e.link(nc.vector.scalar_tensor_tensor(ktmp, d_hi, float(P * NP), d_lo, ALU.mult, ALU.add))
                e.link(nc.vector.scalar_tensor_tensor(ktmp, s_lo, float(NP), ktmp, ALU.mult, ALU.add))
                ins = nc.vector.scalar_tensor_tensor(key, s_hi, float(P), ktmp, ALU.mult, ALU.add)
                e.link(ins)
                if r == 0:
                    dve.sem_inc(key_made, 1)
            e.link(nc.vector.tensor_scalar(dst_lo16, d_lo, 0.0, None, ALU.add))
            e.link(nc.vector.tensor_scalar(dst_hi16, d_hi, 0.0, None, ALU.add))
            dve.sem_inc(ev_lo, 2)
            split_lo(dve, KV_W, slice(0, 2))
            dve.wait_ge(consts, 1)

            def newton(chain, r, v, sd, t):
                chain.link(nc.vector.reciprocal(r, sd))
                chain.link(nc.vector.tensor_tensor(t, r, r, ALU.mult))
                chain.link(nc.vector.tensor_tensor(t, t, v, ALU.mult))
                chain.link(nc.vector.tensor_scalar(t, t, -0.5, 1.5, ALU.mult, ALU.add))
                chain.link(nc.vector.tensor_tensor(r, r, t, ALU.mult))

            halves6 = lambda ap: ap[:, 0:D].rearrange("p (k n) -> p k n", k=K)
            LN1_LINKS = 8
            ln1_base = links(LN1_LINKS, T)

            def evict_lo(n, u):
                dve.wait_ge(tr_done, n + 3)
                apart(dve)
                nc.vector.tensor_copy(xT[1][:, :, bass.ds(n * P, P)], halves6(bank16(2 * u + 1))).then_inc(ev_lo, 1)

            def statistics(n, q, i):
                u = q % 2
                ch = Chain(dve, dve_done, n * LN1_LINKS + (ln1_base - 6) if reused(n) else ln1_base)
                dve.wait_ge(x_ld[q], 16 * i + 16)
                nc.vector.bn_stats(bst[:, u, 0:6], x_in[q][:, 0:HD])
                ch.link(nc.vector.bn_stats(bst[:, u, 6:12], x_in[q][:, HD:D]))
                apart(dve)
                ch.link(nc.vector.bn_aggr(bits[:, u, 4:6], bst[:, u, :]))
                nc.vector.tensor_scalar(bits[:, u, 1:2], bits[:, u, 5:6], LN_EPS, None, ALU.add).then_inc(var_ready, 1)

            def low(n, u):
                dve.wait_ge(hi_ready, n + 1)
                nc.vector.tensor_tensor(xlo[u], xn[u], xhi[u], ALU.subtract).then_inc(lo_ready, 1)

            def ln1(n, q, i):
                u, last = q % 2, isinstance(n, int) and n == T - 1
                if reused(n):
                    low(n - 1, 1 - u)
                if not last:
                    statistics(n + 1, (q + 1) % 4, i + 1 if q == 3 else i)
                ch = Chain(dve, dve_done, n * LN1_LINKS + (ln1_base + (2 if last else 4)))
                dve.wait_ge(sd_ready, n + 1)
                dve.wait_ge(var_ready, n + 1)
                newton(ch, bits[:, u, 2:3], bits[:, u, 1:2], bits[:, u, 0:1], bits[:, u, 3:4])
                if reused(i) or q >= 2:
                    dve.wait_ge(xn_st[u], 32 * i + 16 * (q // 2))
                ch.link(nc.vector.tensor_scalar(xn[u], x_in[q], bits[:, u, 4:5], bits[:, u, 2:3],
                                                ALU.subtract, ALU.mult))
                dve.sem_inc(xn_ready, 1)
                if reused(n):
                    evict_lo(n - 1, 1 - u)
                if isinstance(n, int) and n < 4:
                    split_lo(dve, KV_W, slice(n + 2, n + 3))

            statistics(0, 0, 0)
            over_rows(dve, ln1)
            low(T - 1, 0)
            evict_lo(T - 1, 0)
            finish_phase(dve, 0)

            dve.sem_inc(scan_done, 2)
            dve.sem_inc(kv_free, 1)
            dve.sem_inc(deg_free, 1)
            ch = Chain(dve, dve_done, links(2))
            ch.link(nc.vector.memset(kv, 0.0))
            ch.link(nc.vector.memset(vals, 0.0))
            dve.sem_inc(vals_clear, 1)
            bank_pair = lambda s: pair[s][:, :, 0:HW]
            UNIT_LINKS = 3
            unit_base = links(UNIT_LINKS, UNITS)

            def copy_k(c, p):
                s, j = slot_use[("k", p)]
                dve.wait_ge(slot_full[s], c * uses[s] + j + 1)
                src = bank_pair(s)
                nc.vector.tensor_copy(kk[p % 2][0:DH, 0, :].rearrange("p (a b) -> p a b", a=2), src[0:DH])\
                    .then_inc(kk_cp, 1)
                nc.vector.tensor_copy(kk[p % 2][DH:P, 1, :].rearrange("p (a b) -> p a b", a=2), src[DH:P])\
                    .then_inc(kk_cp, 1)
                dve.wait_ge(kk_cp, 2 * (c * PAIRS + p) + 2)
                dve.sem_inc(slot_free[s], 2)

            def scan(c, p):
                m = c * PAIRS + p
                dve.wait_ge(kb_in[p % 2], 16 * (c * (PAIRS // 2) + p // 2 + 1))
                for j in range(EPU):
                    dve.wait_ge(scan_done, m * EPU + (j + 1))
                    nc.vector.scalar_tensor_tensor(
                        out=junk[j % 2], in0=kb[p % 2][:, (j // G) * G * P:(j // G + 1) * G * P],
                        scalar=kcol[:, bass.ds(m * EPU + j, 1)], in1=earlier[:, j % G, :], op0=ALU.is_equal,
                        op1=ALU.mult, accum_out=sums[:, j:j + 1]).then_inc(scan_done, 1)
                dve.wait_ge(scan_done, m * EPU + (EPU + 2))
                dve.sem_inc(unit_scanned, 1)
                cu = Chain(dve, dve_done, m * UNIT_LINKS + unit_base)
                cu.link(nc.vector.tensor_scalar(skip, sums, EARLIER, FAR, ALU.is_ge, ALU.mult))
                cu.link(nc.vector.tensor_tensor(idx_all[:, bass.ds(m * EPU, EPU)], kcol[:, bass.ds(m * EPU, EPU)],
                                                skip, ALU.add))
                cu.link(nc.vector.tensor_scalar(val_all[:, bass.ds(m * EPU, EPU)], sums, 0.0, None, ALU.add))
                dve.sem_inc(idx_ready, 1)
                iota_b = iota.rearrange("p (o n) -> p o n", o=1).to_broadcast([P, EPU, P])
                nc.vector.tensor_tensor(oh_lo, iota_b, dst_lo16[:, bass.ds(m * EPU, EPU)].rearrange(
                    "p (j o) -> p j o", o=1).to_broadcast([P, EPU, P]), ALU.is_equal).then_inc(oh_ready, 1)
                iota_h = iota[:, 0:26].rearrange("p (o n) -> p o n", o=1).to_broadcast([P, EPU, 26])
                nc.vector.tensor_tensor(oh_hi, iota_h, dst_hi16[:, bass.ds(m * EPU, EPU)].rearrange(
                    "p (j o) -> p j o", o=1).to_broadcast([P, EPU, 26]), ALU.is_equal).then_inc(oh_ready, 1)

            def add_kv(c, p):
                m = c * PAIRS + p
                dve.wait_ge(kv_full, m + 1)
                dst = kv[:, p, :, :].rearrange("p a b -> p (a b)")
                nc.vector.tensor_tensor(dst, dst, bank(6)[:, 0:4 * VW], ALU.add).then_inc(kv_free, 1)
                dve.wait_ge(deg_full, m + 1)
                dve.wait_ge(deg_free, m + 1)
                nc.vector.tensor_tensor(deg, deg, bank(7)[:, 0:26], ALU.add).then_inc(deg_free, 1)

            with dve.Fori(0, C) as c:
                dve.wait_ge(slot_full[0], c * uses[0] + 1)
                apart(dve)
                nc.vector.tensor_tensor(
                    vals[:, :, :, DH], valid[:, bass.ds(c * TC, TC)].rearrange("p (t o) -> p t o", o=1)
                    .to_broadcast([P, TC, H]), ones60.rearrange("p (t h) -> p t h", t=TC), ALU.mult)\
                    .then_inc(vone_ready, 1)
                copy_k(c, 0)
                for p in range(PAIRS):
                    scan(c, p)
                    if p + 1 < PAIRS:
                        copy_k(c, p + 1)
                    add_kv(c, p)
            finish_phase(dve, 1)

            split_lo(dve, Q_W)
            nc.vector.tensor_scalar(kv, kv, 1.0 / M, None, ALU.mult).then_inc(kv_scaled, 1)
            nc.vector.tensor_reduce(flag_f[:, 0:1], deg[:, 0:T], AXX, ALU.max).then_inc(flag_max, 1)
            cs = Chain(dve, dve_done, links(5))
            dve.wait_ge(sq_done, 1)
            newton(cs, dinv, deg[:, 0:T], t25[:, 0, :], t25[:, 2, :])

            def copy_q(c, p):
                dve.wait_ge(qt_full, c * PAIRS + p + 1)
                src = bank_pair(0)
                nc.vector.tensor_copy(kk[p % 2][0:DH, 0, :].rearrange("p (a b) -> p a b", a=2), src[0:DH])\
                    .then_inc(qq_cp, 1)
                nc.vector.tensor_copy(kk[p % 2][DH:P, 1, :].rearrange("p (a b) -> p a b", a=2), src[DH:P])\
                    .then_inc(qq_cp, 1)
                dve.wait_ge(qq_cp, 2 * (c * PAIRS + p) + 2)
                dve.sem_inc(qt_free, 1)

            o_parts = [(0, 3, pair[3][:, 0, 0:3 * 2 * VW].rearrange("p (t h e) -> p t h e", t=3, h=2)),
                       (3, 5, pair[3][:, 1, 0:2 * 2 * VW].rearrange("p (t h e) -> p t h e", t=2, h=2))]

            def normalise(c, p):
                m = c * PAIRS + p
                cn = Chain(dve, dve_done, c * (q_links + y_links) + (q_base + 4 * p))
                dve.wait_ge(o_full, m + 1)
                nc.vector.tensor_scalar(rden[:, 0:3, :], o_parts[0][2][:, :, :, DH], 1e-6, None, ALU.add)
                cn.link(nc.vector.tensor_scalar(rden[:, 3:5, :], o_parts[1][2][:, :, :, DH], 1e-6, None, ALU.add))
                cn.link(nc.vector.reciprocal(rden, rden))
                for a, b, o in o_parts:
                    cn.link(nc.vector.tensor_tensor(
                        attn[:, a:b, p * P:(p + 1) * P].rearrange("p t (h e) -> p t h e", h=2), o[:, :, :, 0:DH],
                        rden[:, a:b, :].rearrange("p t (h o) -> p t h o", o=1).to_broadcast([P, b - a, 2, DH]),
                        ALU.mult))
                dve.sem_inc(attn_done, 1)

            q_links, y_links = 4 * PAIRS, 3 * TC
            q_base = links(q_links + y_links, C)

            def counts(L, n, u):
                dve.wait_ge(L.ahi, n + 1)
                nc.vector.tensor_tensor(a_lo[u].rearrange("p a b -> p (a b)"), a_in[u],
                                        a_hi[u].rearrange("p a b -> p (a b)"), ALU.subtract).then_inc(L.alo, 1)

            def chunk3(c, first=False, more=True):
                for p in range(PAIRS):
                    if p + 1 < PAIRS:
                        copy_q(c, p + 1)
                    if first:
                        split_lo(dve, P_W, slice(p, p + 1))
                    normalise(c, p)
                if first:
                    dve.wait_ge(rows_in, 16)

                def low(t):
                    dve.wait_ge(ahi_ready, c * TC + t + 1)
                    nc.vector.tensor_tensor(alo[t % 2], attn[:, t, :], ahi[t % 2], ALU.subtract).then_inc(alo_ready, 1)

                def rows(t):
                    s, j = q_use[("y", t)]
                    ys, yj = y_use[t]
                    cr = Chain(dve, dve_done, c * (q_links + y_links) + (q_base + q_links + 3 * t))
                    dve.wait_ge(qp_full[s], c * q_uses[s] + j + 1)
                    dve.wait_ge(xl_in[ys], 16 * (c * y_uses[ys] + yj + 1))
                    if reused(c) or yj:
                        dve.wait_ge(y_st[ys], 16 * (c * y_uses[ys] + yj))
                    nc.vector.tensor_tensor(halves(y_sb[ys]), wide(1 + s), halves(xl3[ys]), ALU.add)\
                        .then_inc(xl_used[ys], 1)
                    dve.wait_ge(xl_used[ys], c * y_uses[ys] + yj + 2)
                    dve.sem_inc(qp_free[s], 1)
                    cr.link(nc.vector.tensor_tensor(y_sb[ys], y_sb[ys], brow3, ALU.add))
                    dve.sem_inc(y_ready, 1)
                    nc.vector.bn_stats(bst[:, 0, 0:6], y_sb[ys][:, 0:HD])
                    cr.link(nc.vector.bn_stats(bst[:, 0, 6:12], y_sb[ys][:, HD:D]))
                    apart(dve)
                    cr.link(nc.vector.bn_aggr(mvt[:, t, :], bst[:, 0, :]))

                low(0)
                low(1)
                for t in range(TC):
                    dve.wait_ge(atr_full, c * TC + t + 3)
                    nc.vector.tensor_copy(aT[1][t % 2], bank16(7)[:, 0:D]).then_inc(aT_lo, 1)
                    if t + 2 < TC:
                        low(t + 2)
                    if t == 0 and more:
                        copy_q(c + 1, 0)
                    if t:
                        rows(t - 1)
                    if not more:
                        if t in (1, 3):
                            counts(L1, t // 2, t // 2)
                        if t in (2, 4):
                            split_lo(dve, G1_W, slice(t - 2, t))
                rows(TC - 1)
                nc.vector.tensor_scalar(mvy[:, bass.ds(c * TC, TC), :], mvt, 0.0, None, ALU.add).then_inc(mvy_done, 1)
                dve.wait_ge(mvy_done, c + 1)

            copy_q(0, 0)
            chunk3(0, first=True)
            with dve.Fori(1, C - 1) as c:
                chunk3(c)
            chunk3(C - 1, more=False)
            split_lo(dve, G1_W, slice(4, K))
            cs = Chain(dve, dve_done, links(1))
            dve.wait_ge(flag_max, 2)
            cs.link(nc.vector.tensor_scalar(flag_i, flag_f[:, 1:2].to_broadcast([P, 2]), COUNT_EXACT, None, ALU.is_gt))
            dve.sem_inc(flag_ready, 1)
            finish_phase(dve, 2)

            def pre(n, q, i):
                dve.wait_ge(pre_hi, n + 1)
                row = lambda part: X[part][:, bass.ds(n, 1), :].rearrange("p a b -> p (a b)")
                nc.vector.scalar_tensor_tensor(row(1), xl4[q], dinv[:, bass.ds(n, 1)], row(0),
                                               ALU.mult, ALU.subtract).then_inc(pre_lo, 1)

            def layer(L, first, seg):
                def split_g(n, u):
                    dve.wait_ge(L.ghi, n + 1)
                    nc.vector.tensor_tensor(halves(glo[u]), wide(u), halves(ghi[u]), ALU.subtract).then_inc(L.glo, 1)

                def evict(n, u):
                    dve.wait_ge(L.tr, n + 3)
                    nc.vector.tensor_copy(gT[1][u], bank16(5)[:, 0:D]).then_inc(L.gT_lo, 1)

                def finish1(n, u, i):
                    dve.wait_ge(L.z_full, n + 1)
                    dve.wait_ge(L.relu, n + 1)
                    nc.vector.scalar_tensor_tensor(halves(zt[u]), wide(3), dinv[:, bass.ds(n, 1)], halves(row_a),
                                                   ALU.mult, ALU.add).then_inc(L.z_ev, 1)
                    dve.wait_ge(L.zhi, n + 1)
                    nc.vector.tensor_tensor(zlo[u], zr[u], zhi[u], ALU.subtract).then_inc(L.zlo, 1)

                LINKS = 7
                row_base = 0 if first else links(1)
                l2_base = 0 if first else links(LINKS, T)

                def finish2(n, u, i):
                    cc = Chain(dve, dve_done, n * LINKS + l2_base)
                    dve.wait_ge(L.x_ld[u], 32 * i + 32)
                    cc.link(nc.vector.tensor_scalar(yl[u], yl[u], mvy[:, bass.ds(n, 1), 0], ry[:, bass.ds(n, 1)],
                                                    ALU.subtract, ALU.mult))
                    cc.link(nc.vector.tensor_tensor(yl[u], yl[u], row_g, ALU.mult))
                    cc.link(nc.vector.tensor_tensor(xl[u], xl[u], row_a, ALU.add))
                    cc.link(nc.vector.tensor_tensor(xl[u], xl[u], yl[u], ALU.add))
                    dve.wait_ge(L.z_full, n + 1)
                    if reused(i):
                        dve.wait_ge(L.st[u], 16 * i)
                    cc.link(nc.vector.scalar_tensor_tensor(halves(zt[u]), wide(3), dinv[:, bass.ds(n, 1)],
                                                           halves(xl[u]), ALU.mult, ALU.add))
                    dve.sem_inc(L.z_ev, 1)
                    nc.vector.bn_stats(bst[:, u, 0:6], zt[u][:, 0:HD])
                    cc.link(nc.vector.bn_stats(bst[:, u, 6:12], zt[u][:, HD:D]))
                    apart(dve)
                    cc.link(nc.vector.bn_aggr(mvt[:, u, :], bst[:, u, :]))
                    nc.vector.tensor_scalar(mv2[:, bass.ds(n, 1), :].rearrange("p a b -> p (a b)"), mvt[:, u, :],
                                            0.0, None, ALU.add).then_inc(L.zlo, 1)

                def body(n, u, i, more=True):
                    if more:
                        counts(L, n + 1, 1 - u)
                    if reused(n):
                        evict(n - 1, 1 - u)
                    split_g(n, u)
                    if reused(n):
                        (finish1 if first else finish2)(n - 1, 1 - u, i if u == 1 else i - 1)

                if first:
                    over_rows(dve, pre)
                    cs = Chain(dve, dve_done, links(6))
                    cs.link(nc.vector.tensor_scalar(mvy[:, :, 1], mvy[:, :, 1], LN_EPS, None, ALU.add))
                    dve.sem_inc(sq_asked, 1)
                    dve.wait_ge(sq_done, 2)
                    newton(cs, ry, mvy[:, :, 1], t25[:, 1, :], t25[:, 2, :])
                else:
                    counts(L, 0, 0)
                    counts(L, 1, 1)
                    split_lo(dve, seg)
                if first:
                    dve.wait_ge(rows_in, 32)
                else:
                    dve.wait_ge(rows_in, 80)
                    cb = Chain(dve, dve_done, row_base)
                    cb.link(nc.vector.tensor_tensor(row_a, row_a, row_t, ALU.add))
                body(0, 0, 0, False)
                body(1, 1, 0)
                body(2, 0, 1)
                with dve.Fori(0, (T - 5) // 2) as i:
                    body(2 * i + 3, 1, i + 1)
                    body(2 * i + 4, 0, i + 2)
                body(T - 2, 1, T // 2 - 1)
                body(T - 1, 0, T // 2, False)
                evict(T - 1, 0)
                if not first:
                    split_lo(dve, FIN_W, slice(0, 2))
                (finish1 if first else finish2)(T - 1, 0, (T - 1) // 2)

            layer(L1, True, G1_W)
            finish_phase(dve, 3)
            layer(L2, False, G2_W)
            dve.wait_ge(L2.zlo, T)
            cb = Chain(dve, dve_done, links(6))
            cb.link(nc.vector.tensor_scalar(mv2[:, :, 1], mv2[:, :, 1], LN_EPS, None, ALU.add))
            dve.sem_inc(L2.done, 1)
            dve.wait_ge(sq_done, 3)
            newton(cb, r2, mv2[:, :, 1], t25[:, 0, :], t25[:, 2, :])
            finish_phase(dve, 4)

            FL = 12

            def f_low(n, u, i):
                dve.wait_ge(f_ld[u], 16 * i + 16)
                nc.vector.tensor_scalar(fn[u], fx[u], mv2[:, bass.ds(n, 1), 0], r2[:, bass.ds(n, 1)],
                                        ALU.subtract, ALU.mult).then_inc(f_norm, 1)
                dve.wait_ge(f_hi, n + 1)
                nc.vector.tensor_tensor(flo[u], fn[u], fhi[u], ALU.subtract).then_inc(f_lo, 1)

            def f_evict(n, u):
                dve.wait_ge(f_tr, n + 3)
                nc.vector.tensor_copy(fT[1][u], bank16(1)[:, 0:D]).then_inc(fT_lo, 1)

            f_base = links(FL, T)

            def select(n, u):
                cf = Chain(dve, dve_done, n * FL + f_base)
                dve.wait_ge(f_h, n + 1)
                cf.link(nc.vector.tensor_reduce(nmax[:, 0:1], bank(4)[:, 384:384 + NX], AXX, ALU.max))
                cf.link(nc.vector.tensor_scalar(lg, bank(4)[:, 384:384 + NX], nmax[:, 0:1], -104.0,
                                                ALU.subtract, ALU.max))
                apart(dve)
                cf.link(nc.vector.max(top, lg))
                apart(dve)
                cf.link(nc.vector.max_index(topi, top, lg))
                cf.link(nc.vector.tensor_copy(topf, topi))
                cf.link(nc.vector.tensor_tensor(esel[:, 0:1], topf[:, 0:1], topf[:, 1:2], ALU.max))
                cf.link(nc.vector.tensor_scalar(mask, iota8, esel[:, 0:1], None, ALU.is_equal))
                nc.vector.tensor_scalar(mask16, iota8, esel[:, 0:1], None, ALU.is_equal)
                m3 = mask.rearrange("p (e o) -> p e o", o=1)
                for b in range(2):
                    ins = nc.vector.tensor_tensor(
                        hsel_all[:, 4 * b:4 * b + 4, :], bank(2 + b).rearrange("p (e i) -> p e i", e=4),
                        m3[:, 4 * b:4 * b + 4].to_broadcast([P, 4, NI]), ALU.mult)
                cf.link(ins)
                nc.vector.tensor_reduce(hsel, hsel_all.rearrange("p e i -> p i e"), AXX, ALU.add).then_inc(f_hsel, 1)
                dve.wait_ge(f_ahi, n + 1)
                cf.link(nc.vector.tensor_tensor(act_lo, hact, act_hi, ALU.subtract))
                k3 = mask16.rearrange("p (e o) -> p e o", o=1).to_broadcast([P, NX, NI])
                for part, dst in ((act_hi, m_hi), (act_lo, m_lo)):
                    ins = nc.vector.tensor_tensor(
                        dst, part.rearrange("p (o i) -> p o i", o=1).to_broadcast([P, NX, NI]), k3, ALU.mult)
                    cf.link(ins)
                dve.sem_inc(f_mask, 1)
                cf.link(nc.vector.tensor_scalar(topf[:, 0:1], topf[:, 0:1], 0.0, None, ALU.add))
                assert cf.n == FL

            def m_evict(n, u):
                dve.wait_ge(f_mtr, n + 1)
                nc.vector.tensor_copy(mT[1][u], bank16(1)).then_inc(mT_lo, 1)

            def finish(n, u, i):
                dve.wait_ge(f_y, n + 1)
                dve.wait_ge(fr_ld[u], 16 * i + 16)
                if reused(i):
                    dve.wait_ge(f_st[u], 16 * i)
                nc.vector.tensor_tensor(halves(fo[u]), wide(3), halves(fr[u]), ALU.add).then_inc(f_out, 1)

            f_low(0, 0, 0)
            split_lo(dve, FIN_W, slice(2, K))
            f_evict(0, 0)
            split_lo(dve, FOUT_W)

            def experts(n, u, i):
                f_low(n + 1, 1 - u, i if u == 0 else i + 1)
                f_evict(n + 1, 1 - u)
                select(n, u)
                if reused(n):
                    finish(n - 1, 1 - u, i if u == 1 else i - 1)
                m_evict(n, u)

            over_tiles(dve, experts, T - 2)
            for n in (T - 2, T - 1):
                u = n % 2
                if n + 1 < T:
                    f_low(n + 1, 1 - u, (n + 1) // 2)
                    f_evict(n + 1, 1 - u)
                select(n, u)
                finish(n - 1, 1 - u, (n - 1) // 2)
                m_evict(n, u)
            finish(T - 1, 0, (T - 1) // 2)

        @block.tensor
        def _(pe):
            spacer[pe] = sem("pe_spacer")
            pe.wait_ge(consts, 1)
            pe.sem_inc(tr_done, 2)

            def turn(dst_hi, dst_lo, hi, lo, cols=K):
                for dst, part in ((dst_hi, hi), (dst_lo, lo)):
                    for k in range(cols):
                        ins = nc.tensor.transpose(dst[:, k * P:(k + 1) * P], part[:, k * P:(k + 1) * P], ident)
                return ins

            def tr1(n, u, i):
                pe.wait_ge(lo_ready, n + 1)
                pe.wait_ge(ev_hi, n + 1)
                pe.wait_ge(ev_lo, n + 1)
                turn(bank16(2 * u), bank16(2 * u + 1), xhi[u], xlo[u]).then_inc(tr_done, 1)

            over_tiles(pe, tr1)
            finish_phase(pe, 0)

            def node_cols(c, t):
                return lambda k, part: xT[part][:, k, bass.ds(c * CW + t * P, P)]

            def chunk_cols(c):
                return lambda k, part, half: xT[part][:, k, bass.ds(c * CW + half * HW, HW)]

            def k_up(c, p):
                s, j = slot_use[("k", p)]
                pe.wait_ge(slot_free[s], 2 * (c * uses[s] + j) + 2)
                apart(pe)
                for k in range(K):
                    ins = mm_split(bank_halves(s, HW), lambda k, a: kv_w(k, a)[:, p * P:(p + 1) * P],
                                   chunk_cols(c), k, k == 0, k == K - 1)
                ins.then_inc(slot_full[s], 1)

            def k_features(c, p, t):
                n = p * TC + t
                if t == 0:
                    pe.wait_ge(kk_cp, 2 * (c * PAIRS + p) + 2)
                    pe.wait_ge(kk_sq, 2 * (c * PAIRS + p) + 2)
                pe.wait_ge(kp_exp, c * (PAIRS * TC) + n + 1)
                for h in range(2):
                    ins = nc.tensor.matmul(bank(4 + n % 2)[:, h * M:(h + 1) * M],
                                           kk[p % 2][:, h, t * P:(t + 1) * P], (rfa, rfb)[h], start=True, stop=True)
                ins.then_inc(kp_full, 1)

            def k_sums(c, p, t):
                n = p * TC + t
                if t == 0:
                    pe.wait_ge(kv_free, c * PAIRS + p + 1)
                pe.wait_ge(kp_exp, c * (PAIRS * TC) + n + 3)
                for g in range(4):
                    h, half = g // 2, g % 2
                    ins = nc.tensor.matmul(bank(6)[:, g * VW:(g + 1) * VW],
                                           kp_sb[n % 2][:, h * M + half * P:h * M + (half + 1) * P],
                                           vals[:, t, 2 * p + h, :], start=(t == 0 and g == 0), stop=(t == TC - 1),
                                           skip_group_check=True)
                if t == TC - 1:
                    ins.then_inc(kv_full, 1)

            def degrees(c, p):
                m = c * PAIRS + p
                pe.wait_ge(oh_ready, 2 * m + 2)
                pe.wait_ge(deg_free, m + 1)
                for j in range(EPU):
                    ins = nc.tensor.matmul(bank(7)[:, 0:26], oh_lo[:, j, :], oh_hi[:, j, :], start=(j == 0),
                                           stop=(j == EPU - 1))
                ins.then_inc(deg_full, 1)

            weights_ready(pe, KV_W)
            with pe.Fori(0, C) as c:
                for t in range(TC):
                    s, j = slot_use[("v", t)]
                    pe.wait_ge(slot_free[s], 2 * (c * uses[s] + j) + 2)
                    apart(pe)
                    for k in range(K):
                        ins = mm_split(bank_halves(s, HD), node_cols(c, t),
                                       lambda k, b, half: kv_w(k, b)[:, D + half * HD:D + (half + 1) * HD],
                                       k, k == 0, k == K - 1)
                    ins.then_inc(slot_full[s], 1)
                k_up(c, 0)
                pe.wait_ge(vone_ready, c + 1)
                for p in range(PAIRS):
                    k_features(c, p, 0)
                    k_features(c, p, 1)
                    if p + 1 < PAIRS:
                        k_up(c, p + 1)
                    if p == 0:
                        pe.wait_ge(slot_free[0], 2 * (c * uses[0]) + 8)
                        pe.wait_ge(slot_free[1], 2 * (c * uses[1]) + 6)
                    for t in range(TC):
                        k_sums(c, p, t)
                        if t + 2 < TC:
                            k_features(c, p, t + 2)
                    degrees(c, p)
            finish_phase(pe, 1)

            pe.sem_inc(atr_full, 2)
            weights_ready(pe, Q_W)
            pe.sem_inc(L1.g_full, 2)
            pe.sem_inc(L1.tr, 2)
            pe.sem_inc(L2.g_full, 2)
            pe.sem_inc(L2.tr, 2)
            pe.wait_ge(kv_scaled, 1)

            def q_up(c, p):
                pe.wait_ge(qt_free, c * PAIRS + p + 1)
                apart(pe)
                for k in range(K):
                    ins = mm_split(bank_halves(0, HW), lambda k, a: q_w(k, a)[:, p * P:(p + 1) * P],
                                   chunk_cols(c), k, k == 0, k == K - 1)
                ins.then_inc(qt_full, 1)

            def chunk3(c, more=True):
                for p in range(PAIRS):
                    m = c * PAIRS + p
                    pe.wait_ge(qq_cp, 2 * m + 2)
                    pe.wait_ge(qq_sq, 2 * m + 2)
                    for g in range(4):
                        h, half = g // 2, g % 2
                        s, j = q_use[("q", p, g)]
                        pe.wait_ge(qp_free[s], c * q_uses[s] + j + 1)
                        for b in range(2):
                            ins = nc.tensor.matmul(pair[1 + s][:, b, 0:HW], (rfa, rfb)[h][:, half * P:(half + 1) * P],
                                                   kk[p % 2][:, h, b * HW:(b + 1) * HW], start=True, stop=True)
                        ins.then_inc(qp_full[s], 1)
                    if p + 1 < PAIRS:
                        q_up(c, p + 1)
                    pe.wait_ge(qp_exp, m + 1)
                    if p:
                        pe.wait_ge(attn_done, m)
                    for t in range(TC):
                        for h in range(2):
                            o = pair[3][:, t // 3, (t % 3 * 2 + h) * VW:(t % 3 * 2 + h + 1) * VW]
                            for half in range(2):
                                ins = nc.tensor.matmul(o, qp_sb[p % 2][:, 2 * h + half, t * P:(t + 1) * P],
                                                       kv[:, p, 2 * h + half, :], start=(half == 0), stop=(half == 1))
                    ins.then_inc(o_full, 1)

                def turn_a(t):
                    pe.wait_ge(alo_ready, c * TC + t + 1)
                    if t:
                        pe.wait_ge(aT_hi, c * TC + t)
                        pe.wait_ge(aT_lo, c * TC + t)
                    turn(bank16(6), bank16(7), ahi[t % 2], alo[t % 2]).then_inc(atr_full, 1)

                if more:
                    q_up(c + 1, 0)
                turn_a(0)
                for t in range(TC):
                    if t + 1 < TC:
                        turn_a(t + 1)
                    else:
                        pe.wait_ge(aT_hi, c * TC + t + 1)
                        pe.wait_ge(aT_lo, c * TC + t + 1)
                    s, j = q_use[("y", t)]
                    weights_ready(pe, P_W)
                    pe.wait_ge(qp_free[s], c * q_uses[s] + j + 1)
                    for k in range(K):
                        ins = mm_split(bank_halves(1 + s, HD), lambda k, a: aT[a][t % 2][:, k * P:(k + 1) * P],
                                       lambda k, b, half: p_w(k, b)[:, half * HD:(half + 1) * HD],
                                       k, k == 0, k == K - 1)
                    ins.then_inc(qp_full[s], 1)

            q_up(0, 0)
            with pe.Fori(0, C - 1) as c:
                chunk3(c)
            chunk3(C - 1, more=False)
            finish_phase(pe, 2)

            pe.wait_ge(flag_ready, 1)
            large = pe.value_load(flag_i[0:1, 0:1], min_val=0, max_val=1)

            def layer(L, seg, rows):
                def add_rows(u, s):
                    for part in range(2):
                        for half in range(2):
                            ins = nc.tensor.matmul(pair[u][:, half, 0:HD], a_hi[u][:, s, :],
                                                   X[part][:, s, half * HD:(half + 1) * HD],
                                                   start=(s == 0 and part == 0),
                                                   stop=(s == T - 1 and part == 1), skip_group_check=True)
                    return ins

                def add_low(*slots):
                    with pe.If(large):
                        for u in slots:
                            for s in range(T):
                                for half in range(2):
                                    nc.tensor.matmul(pair[u][:, half, 0:HD], a_lo[u][:, s, :],
                                                     X[0][:, s, half * HD:(half + 1) * HD], start=False,
                                                     stop=False, skip_group_check=True)

                def turn_g(n, u):
                    pe.wait_ge(L.glo, n + 1)
                    turn(bank16(4), bank16(5), ghi[u], glo[u]).then_inc(L.tr, 1)

                def gather_two():
                    pe.wait_ge(L.alo, 2)
                    for s in range(T):
                        rows(s)
                        if s == T - 1:
                            add_low(0, 1)
                        for u in range(2):
                            ins = add_rows(u, s)
                            if s == T - 1:
                                ins.then_inc(L.g_full, 1)

                def gather(n, u):
                    pe.wait_ge(L.alo, n + 1)
                    for s in range(T):
                        if s == T // 2:
                            turn_g(n - 1, 1 - u)
                        if s == T - 1:
                            add_low(u)
                        ins = add_rows(u, s)
                    ins.then_inc(L.g_full, 1)

                def gather_third():
                    pe.wait_ge(L.alo, 3)
                    pe.wait_ge(L.glo, 1)
                    for s in range(T):
                        if s == T // 3:
                            turn_g(0, 0)
                        if s == 2 * T // 3:
                            pe.wait_ge(L.gT_hi, 1)
                            pe.wait_ge(L.gT_lo, 1)
                            turn_g(1, 1)
                            transform(0, 0, True)
                        if s == T - 1:
                            add_low(0)
                        ins = add_rows(0, s)
                    ins.then_inc(L.g_full, 1)

                def transform(n, u, first=False):
                    pe.wait_ge(L.gT_hi, n + 1)
                    pe.wait_ge(L.gT_lo, n + 1)
                    if not first:
                        pe.wait_ge(L.z_ev, n)
                    for k in range(K):
                        ins = mm_split(bank_halves(3, HD), lambda k, a: gT[a][u][:, k * P:(k + 1) * P],
                                       lambda k, b, half: gnn_w(k, b)[:, half * HD:(half + 1) * HD],
                                       k, k == 0, k == K - 1)
                    ins.then_inc(L.z_full, 1)

                gather_two()
                weights_ready(pe, seg)
                gather_third()
                transform(1, 1)
                with pe.Fori(0, (T - 3) // 2) as i:
                    gather(2 * i + 3, 1)
                    transform(2 * i + 2, 0)
                    gather(2 * i + 4, 0)
                    transform(2 * i + 3, 1)
                turn_g(T - 1, 0)
                transform(T - 1, 0)

            layer(L1, G1_W, lambda s: pe.wait_ge(pre_lo, s + 1))
            finish_phase(pe, 3)
            layer(L2, G2_W, lambda s: pe.wait_ge(X_in[s // TC], 32) if s % TC == 0 else None)
            finish_phase(pe, 4)

            pe.sem_inc(f_tr, 2)

            def f_turn(n, u):
                pe.wait_ge(f_lo, n + 1)
                turn(bank16(0), bank16(1), fhi[u], flo[u]).then_inc(f_tr, 1)

            def f_up(n, u):
                pe.wait_ge(fT_hi, n + 1)
                pe.wait_ge(fT_lo, n + 1)
                for k in range(K):
                    for m, (a, b) in enumerate(((0, 0), (0, 1), (1, 0))):
                        for dst, lo, hi in ((bank(2), 0, 512), (bank(3), 512, 1024), (bank(4)[:, 384:384 + NX], HB, HB + NX)):
                            ins = nc.tensor.matmul(dst, fT[a][u][:, k * P:(k + 1) * P], w_in(k, b)[:, lo:hi],
                                                   start=(k == 0 and m == 0), stop=(k == K - 1 and m == 2))
                ins.then_inc(f_h, 1)

            def f_mturn(n, u):
                pe.wait_ge(f_mask, n + 1)
                turn(bank16(0), bank16(1), m_hi.rearrange("p e i -> p (e i)"), m_lo.rearrange("p e i -> p (e i)"), NX)\
                    .then_inc(f_mtr, 1)

            def f_down(n, u, first=False):
                pe.wait_ge(mT_hi, n + 1)
                pe.wait_ge(mT_lo, n + 1)
                if not first:
                    pe.wait_ge(f_out, n)
                for e in range(NX):
                    ins = mm_split(bank_halves(3, HD), lambda e, a: mT[a][u][:, e * P:(e + 1) * P],
                                   lambda e, b, half: w_out(e, b)[:, half * HD:(half + 1) * HD],
                                   e, e == 0, e == NX - 1)
                ins.then_inc(f_y, 1)

            f_turn(0, 0)
            weights_ready(pe, FIN_W)
            f_up(0, 0)
            f_turn(1, 1)
            f_mturn(0, 0)
            f_up(1, 1)
            pe.wait_ge(mT_hi, 1)
            pe.wait_ge(mT_lo, 1)
            f_turn(2, 0)
            weights_ready(pe, FOUT_W)
            f_down(0, 0, True)
            f_mturn(1, 1)

            def f_body(n, u):
                f_up(n, u)
                pe.wait_ge(mT_hi, n)
                pe.wait_ge(mT_lo, n)
                f_turn(n + 1, 1 - u)
                f_down(n - 1, 1 - u)
                f_mturn(n, u)

            with pe.Fori(0, (T - 3) // 2) as i:
                f_body(2 * i + 2, 0)
                f_body(2 * i + 3, 1)
            f_up(T - 1, 0)
            f_down(T - 2, 1)
            f_mturn(T - 1, 0)
            f_down(T - 1, 0)


def kernel(**inputs):
    import numpy as _np
    import concourse.bacc as _bacc
    from concourse.bass_utils import run_bass_kernel_spmd as _run

    a = {k: _np.asarray(v) for k, v in inputs.items()}
    x = _np.zeros((NP, D), _np.float32)
    x[:N] = a["x"]
    loops = _np.arange(NP, dtype=_np.int32)
    pad = _np.full(ET * P - E - NP, NP - 1, _np.int32)
    src = _np.concatenate([a["src"].astype(_np.int32), loops, pad])
    dst = _np.concatenate([a["dst"].astype(_np.int32), loops, pad])
    arrays = {
        "x": x,
        "src_row": src.reshape(P, ET), "dst_row": dst.reshape(P, ET),
        "src_col": src.reshape(ET, P).T, "dst_col": dst.reshape(ET, P).T,
        "w_qkv": a["L0_mix_W_qkv"], "w_proj": a["L0_mix_W_proj"],
        "b_proj": a["L0_mix_b_proj"].reshape(1, D), "gamma": a["L0_mix_gamma"].reshape(1, D),
        "beta": a["L0_mix_beta"].reshape(1, D), "rf_t": a["L0_mix_random_features"].T,
        "g1_t": a["L0_gnn_W1"].T, "b1": a["L0_gnn_b1"].reshape(1, D),
        "g2_t": a["L0_gnn_W2"].T, "b2": a["L0_gnn_b2"].reshape(1, D),
        "ffn_in": _np.concatenate([a["L0_ffn_w1"].transpose(1, 0, 2).reshape(D, HB), a["L0_ffn_router_w"].T], axis=1),
        "ffn_out": a["L0_ffn_w2"].reshape(HB, D),
    }
    arrays = {f"in_{k}": _np.ascontiguousarray(v) for k, v in arrays.items()}
    nc = _bacc.Bacc("TRN2", target_bir_lowering=False, num_devices=1)
    args = {k[3:]: nc.dram_tensor(k, v.shape, mybir.dt.from_np(v.dtype), kind="ExternalInput").ap()
            for k, v in arrays.items()}
    out = nc.dram_tensor("out_rows", (NP, D), F32, kind="ExternalOutput").ap()
    build(nc, out=out, **args)
    r = _run(nc, [arrays], core_ids=[0])
    return r.results[0]["out_rows"][:N]
```
